# Optimizing a Trainium2 kernel written in Bass

```python
import numpy as np
import jax
import jax.numpy as jnp

def _softmax(x, axis=-1):
    return jax.nn.softmax(x, axis=axis)

def _gelu(x):
    return jax.nn.gelu(x, approximate=True)

def _silu(x):
    return jax.nn.silu(x)

def _sigmoid(x):
    return jax.nn.sigmoid(x)

def _layernorm(x, axis=-1, eps=1e-05):
    m = jnp.mean(x, axis=axis, keepdims=True)
    v = jnp.var(x, axis=axis, keepdims=True)
    return (x - m) / jnp.sqrt(v + eps)

def _scatter_add(tgt, idx, src, axis=0):
    return tgt.at[idx].add(src)

def _segment_sum(src, seg, n):
    return jax.ops.segment_sum(src, seg, n)
kernel_name = 'mk_flamingo_gated_d1_seqx_r4_3154fa'

def setup_inputs(seed: int=0):
    np.random.seed(seed)
    _w = jnp.asarray

    def _rec_inputs():
        import jax
        import jax.numpy as jnp
        _rk = jax.random.key(seed)
        x = -0.0005146 + 1 * jax.random.normal(jax.random.fold_in(_rk, 1), (16, 256, 256), jnp.float32)
        _lenS = 256 - jax.random.randint(jax.random.fold_in(_rk, 7), (16,), 0, max(1, 256 // 4) + 1, jnp.int32)
        _lenS2 = 77 - jax.random.randint(jax.random.fold_in(_rk, 8), (16,), 0, max(1, 77 // 4) + 1, jnp.int32)
        _ctx_1024P = jax.random.normal(jax.random.fold_in(_rk, 11), (16, 16, 256), jnp.float32)
        _ctx_1024c = jax.random.dirichlet(jax.random.fold_in(_rk, 511), 0.3 * jnp.ones((16,), jnp.float32), (16, 77))
        _ctx_1024t = jnp.einsum('bsk,bkd->bsd', _ctx_1024c, _ctx_1024P)
        _ctx_1024t = _ctx_1024t * jax.lax.rsqrt(jnp.mean(jnp.square(_ctx_1024t)) + 1e-12) * 0.953939
        ctx_1024 = -0.000392918 + 0.999932 * (_ctx_1024t + 0.3 * jax.random.normal(jax.random.fold_in(_rk, 611), (16, 77, 256), jnp.float32))
        _g = jax.random.normal(jax.random.fold_in(_rk, 9001), (2, 1), jnp.float32)
        _g = jnp.sign(_g) * jnp.maximum(jnp.abs(_g), 1.0) + (_g == 0) * 1.0
        g_xattn = _g[0]
        g_ffn = _g[1]
        return (x, ctx_1024, g_xattn, g_ffn)
    x, ctx_1024, g_xattn, g_ffn = _rec_inputs()

    def _L0_xattn_setup():
        import jax, jax.numpy as jnp
        import numpy as np
        DIM = 256
        DIM_HEAD = 64
        HEADS = 16
        INNER = DIM_HEAD * HEADS
        EPS = 1e-05

        def layer_norm(x, g, b):
            m = jnp.mean(x, axis=-1, keepdims=True)
            v = jnp.mean(jnp.square(x - m), axis=-1, keepdims=True)
            return (x - m) * jax.lax.rsqrt(v + EPS) * g + b
        key = jax.random.key(seed)
        ks = jax.random.split(key, 8)
        B, N_IMG, N_LAT = (4, 1024, 128)
        std = 1.0 / np.sqrt(DIM)
        return {'image_embeds': jax.random.normal(ks[0], (B, N_IMG, DIM), dtype=jnp.float32), 'latents': jax.random.normal(ks[1], (B, N_LAT, DIM), dtype=jnp.float32), 'ln1_g': jnp.ones((DIM,), jnp.float32), 'ln1_b': jnp.zeros((DIM,), jnp.float32), 'ln2_g': jnp.ones((DIM,), jnp.float32), 'ln2_b': jnp.zeros((DIM,), jnp.float32), 'Wq': jax.random.normal(ks[2], (DIM, INNER), dtype=jnp.float32) * std, 'Wkv': jax.random.normal(ks[3], (DIM, 2 * INNER), dtype=jnp.float32) * std, 'Wo': jax.random.normal(ks[4], (INNER, DIM), dtype=jnp.float32) * std}
    _L0_xattn_all = _L0_xattn_setup()
    _L0_xattn_in = {k: v for k, v in _L0_xattn_all.items() if k in ('ln1_g', 'ln1_b', 'ln2_g', 'ln2_b', 'Wq', 'Wkv', 'Wo')}
    del _L0_xattn_all

    def _L0_ffn_setup():
        import jax, jax.numpy as jnp
        import numpy as np
        B, S, H, I, E, TOPK, KS = (4, 1024, 256, 128, 16, 2, 3)
        key = jax.random.key(seed)
        ks = jax.random.split(key, 9)
        sc = 0.02
        return {'hidden_states': jax.random.normal(ks[0], (B, S, H), dtype=jnp.float32), 'router_w': jax.random.normal(ks[1], (H, E), dtype=jnp.float32) * sc, 'router_bias': jnp.zeros((E,), dtype=jnp.float32), 'expert_gate_w': jax.random.normal(ks[2], (E - 1, H, I), dtype=jnp.float32) * sc, 'expert_up_w': jax.random.normal(ks[3], (E - 1, H, I), dtype=jnp.float32) * sc, 'expert_down_w': jax.random.normal(ks[4], (E - 1, I, H), dtype=jnp.float32) * sc, 'conv_w': jax.random.normal(ks[5], (I, H, KS), dtype=jnp.float32) * sc, 'shared_up_w': jax.random.normal(ks[6], (H, I), dtype=jnp.float32) * sc, 'shared_down_w': jax.random.normal(ks[7], (I, H), dtype=jnp.float32) * sc}
    _L0_ffn_all = _L0_ffn_setup()
    _L0_ffn_in = {k: v for k, v in _L0_ffn_all.items() if k in ('router_w', 'router_bias', 'expert_gate_w', 'expert_up_w', 'expert_down_w', 'conv_w', 'shared_up_w', 'shared_down_w')}
    del _L0_ffn_all
    return {'x': x, 'ctx_1024': ctx_1024, 'g_xattn': g_xattn, 'g_ffn': g_ffn, 'L0_xattn_ln1_g': _L0_xattn_in['ln1_g'], 'L0_xattn_ln1_b': _L0_xattn_in['ln1_b'], 'L0_xattn_ln2_g': _L0_xattn_in['ln2_g'], 'L0_xattn_ln2_b': _L0_xattn_in['ln2_b'], 'L0_xattn_Wq': _L0_xattn_in['Wq'], 'L0_xattn_Wkv': _L0_xattn_in['Wkv'], 'L0_xattn_Wo': _L0_xattn_in['Wo'], 'L0_ffn_router_w': _L0_ffn_in['router_w'], 'L0_ffn_router_bias': _L0_ffn_in['router_bias'], 'L0_ffn_expert_gate_w': _L0_ffn_in['expert_gate_w'], 'L0_ffn_expert_up_w': _L0_ffn_in['expert_up_w'], 'L0_ffn_expert_down_w': _L0_ffn_in['expert_down_w'], 'L0_ffn_conv_w': _L0_ffn_in['conv_w'], 'L0_ffn_shared_up_w': _L0_ffn_in['shared_up_w'], 'L0_ffn_shared_down_w': _L0_ffn_in['shared_down_w']}

def reference(x, ctx_1024, g_xattn, g_ffn, L0_xattn_ln1_g, L0_xattn_ln1_b, L0_xattn_ln2_g, L0_xattn_ln2_b, L0_xattn_Wq, L0_xattn_Wkv, L0_xattn_Wo, L0_ffn_router_w, L0_ffn_router_bias, L0_ffn_expert_gate_w, L0_ffn_expert_up_w, L0_ffn_expert_down_w, L0_ffn_conv_w, L0_ffn_shared_up_w, L0_ffn_shared_down_w):
    import jax
    import jax.numpy as jnp

    def _L0_xattn_ref(image_embeds, latents, ln1_g, ln1_b, ln2_g, ln2_b, Wq, Wkv, Wo):
        import jax, jax.numpy as jnp
        import numpy as np
        DIM = 256
        DIM_HEAD = 64
        HEADS = 16
        INNER = DIM_HEAD * HEADS
        EPS = 1e-05

        def layer_norm(x, g, b):
            m = jnp.mean(x, axis=-1, keepdims=True)
            v = jnp.mean(jnp.square(x - m), axis=-1, keepdims=True)
            return (x - m) * jax.lax.rsqrt(v + EPS) * g + b
        B, S_lat, _ = latents.shape
        x = layer_norm(image_embeds, ln1_g, ln1_b)
        l = layer_norm(latents, ln2_g, ln2_b)
        q = l @ Wq
        kv_in = jnp.concatenate([x, l], axis=1)
        kv = kv_in @ Wkv
        k, v = jnp.split(kv, 2, axis=-1)

        def to_heads(t):
            return t.reshape(t.shape[0], t.shape[1], HEADS, DIM_HEAD).transpose(0, 2, 1, 3)
        q, k, v = (to_heads(q), to_heads(k), to_heads(v))
        scale = 1.0 / np.sqrt(np.sqrt(DIM_HEAD))
        w = jnp.einsum('bhqd,bhkd->bhqk', q * scale, k * scale)
        w = jax.nn.softmax(w.astype(jnp.float32), axis=-1).astype(q.dtype)
        out = jnp.einsum('bhqk,bhkd->bhqd', w, v)
        out = out.transpose(0, 2, 1, 3).reshape(B, S_lat, INNER)
        return out @ Wo

    def _L0_ffn_ref(hidden_states, router_w, router_bias, expert_gate_w, expert_up_w, expert_down_w, conv_w, shared_up_w, shared_down_w):
        import jax, jax.numpy as jnp
        import numpy as np
        B, S, H, I, E, TOPK, KS = (4, 1024, 256, 128, 16, 2, 3)
        b, s, h = hidden_states.shape
        flat = hidden_states.reshape(b * s, h)
        logits = (flat @ router_w).astype(jnp.float32) + router_bias
        probs = jax.nn.softmax(logits, axis=-1)
        top_w, top_i = jax.lax.top_k(probs, TOPK)
        norm_w = top_w / (jnp.sum(top_w, axis=-1, keepdims=True) + 1e-06)
        norm_w = norm_w.astype(hidden_states.dtype)
        combine = jnp.sum(jax.nn.one_hot(top_i, E, dtype=norm_w.dtype) * norm_w[..., None], axis=1)
        routed = combine[:, E - 1:E] * flat
        for e in range(E - 1):
            y = jax.nn.silu(flat @ expert_gate_w[e]) * (flat @ expert_up_w[e]) @ expert_down_w[e]
            routed = routed + combine[:, e:e + 1] * y
        routed = routed.reshape(b, s, h)
        x_ncw = jnp.transpose(hidden_states, (0, 2, 1))
        gate = jax.lax.conv_general_dilated(x_ncw, conv_w, window_strides=(1,), padding=[(KS - 1, 0)], dimension_numbers=('NCW', 'OIW', 'NCW'))
        gate = jnp.transpose(gate, (0, 2, 1))
        shared = jax.nn.silu(gate) * (hidden_states @ shared_up_w) @ shared_down_w
        return shared + routed
    x = x + jnp.tanh(g_xattn[0]) * _L0_xattn_ref(ctx_1024, _layernorm(x, axis=-1), L0_xattn_ln1_g, L0_xattn_ln1_b, L0_xattn_ln2_g, L0_xattn_ln2_b, L0_xattn_Wq, L0_xattn_Wkv, L0_xattn_Wo)
    x = x + jnp.tanh(g_ffn[0]) * _L0_ffn_ref(_layernorm(x, axis=-1), L0_ffn_router_w, L0_ffn_router_bias, L0_ffn_expert_gate_w, L0_ffn_expert_up_w, L0_ffn_expert_down_w, L0_ffn_conv_w, L0_ffn_shared_up_w, L0_ffn_shared_down_w)
    return x

_drawn_inputs = setup_inputs


def setup_inputs(seed=0):
    import zlib

    import numpy as np

    out = dict(_drawn_inputs(seed))
    spreads = {'L0_xattn_ln1_g': (1.0, 0.2),
     'L0_xattn_ln1_b': (0.0, 0.1),
     'L0_xattn_ln2_g': (1.0, 0.2),
     'L0_xattn_ln2_b': (0.0, 0.1),
     'L0_ffn_router_bias': (0.0, 0.1)}
    factors = {'L0_ffn_expert_gate_w': 7.412,
     'L0_ffn_expert_up_w': 7.301,
     'L0_ffn_expert_down_w': 7.325,
     'L0_ffn_conv_w': 2.875,
     'L0_ffn_shared_up_w': 2.791,
     'L0_ffn_shared_down_w': 2.795}
    for name, (base, spread) in spreads.items():
        noise = np.random.default_rng([zlib.crc32(name.encode()), seed]).standard_normal(out[name].shape)
        drawn = base * np.exp(spread * noise) if base else spread * noise
        out[name] = jnp.asarray(drawn.astype(out[name].dtype))
    for name, factor in factors.items():
        out[name] = (out[name] * factor).astype(out[name].dtype)
    return out
```

```python
from contextlib import ExitStack

import concourse.bass as bass
from concourse import mybir

F32 = mybir.dt.float32
F32R = mybir.dt.float32r
ACT = mybir.ActivationFunctionType
ALU = mybir.AluOpType
AX = mybir.AxisListType

P = 128
HALF = P // 2


def constants(nc, sb, sem, block_of):
    pass


def build(nc, x, ctx_in, g_xattn, g_ffn, ln1_g, ln1_b, ln2_g, ln2_b, Wq, Wkv, Wo,
          router_w, router_bias, gate_w, up_w, down_w, conv_w, sh_up, sh_down, out):
    B, SQ, D = x.shape
    SC = ctx_in.shape[1]
    INNER = Wq.shape[1]
    DH = HALF
    H = INNER // DH
    PAIRS = H // 2
    KD = D // P
    QT = SQ // P
    NT = B * QT
    SKV = SQ + SC
    SKVE = SKV + SKV % 2
    KT = [(i * P, min(P, SKV - i * P)) for i in range((SKV + P - 1) // P)]
    NKT = len(KT)
    EPS = 1e-5
    SCALE = 1.0 / float(DH) ** 0.5
    assert NKT == 3 and KD == 2 and QT == 2

    with ExitStack() as keep:
        X = keep.enter_context(nc.sbuf_tensor("X", [P, NT, D], F32))
        ident = keep.enter_context(nc.sbuf_tensor("ident", [P, P], F32))
        tanh_g = keep.enter_context(nc.sbuf_tensor("tanh_g", [P, 2], F32))
        E = router_w.shape[1]
        TILES = (2 * B * SQ + E * (P - 1)) // P
        TILES += TILES % 2
        slots_x = nc.dram_tensor("slots_x", (TILES * P, D), F32, kind="Internal").ap()
        slots_y = nc.dram_tensor("slots_y", (TILES * P, D), F32, kind="Internal").ap()
        attention(nc, X, ident, tanh_g, x, ctx_in, g_xattn, g_ffn, ln1_g, ln1_b, ln2_g, ln2_b,
                  Wq, Wkv, Wo, slots_x, locals())
        experts(nc, X, ident, tanh_g, router_w, router_bias, gate_w, up_w, down_w, conv_w,
                sh_up, sh_down, slots_x, slots_y, out, locals())


def experts(nc, X, ident, tanh_g, router_w, router_bias, gate_w, up_w, down_w, conv_w,
            sh_up, sh_down, slots_x, slots_y, out, s):
    B, SQ, D, KD, QT, NT, EPS, E, TILES = (
        s[n] for n in "B SQ D KD QT NT EPS E TILES".split())
    NE = gate_w.shape[0]
    I = gate_w.shape[2]
    KS_ = conv_w.shape[2]
    PAD = KS_ - 1
    U32 = mybir.dt.uint32
    I32 = mybir.dt.int32
    assert I == P and NT * E == 512

    with ExitStack() as c:
        def sb(name, shape, dt=F32):
            return c.enter_context(nc.sbuf_tensor(name, shape, dt))

        def sem(name):
            return c.enter_context(nc.semaphore(name))

        def banks(name, n):
            return [c.enter_context(nc.psum_tensor(f"{name}{i}", [P, 512], F32)) for i in range(n)]

        w_gu = sb("w_gu", [P, NE, KD, 2, I])
        w_dn = sb("w_dn", [P, NE, D])
        conv_raw = sb("conv_raw", [P, D, KS_])
        w_cv = sb("w_cv", [P, KS_, KD, I])
        w_su = sb("w_su", [P, KD, I])
        w_sd = sb("w_sd", [P, D])
        w_rt = sb("w_rt", [P, KD, E])
        bias = sb("bias", [P, E])
        hid = sb("hid", [P, NT, D])
        hT = sb("hT", [P, 2, KD, PAD + SQ])
        h_row = sb("h_row", [P, 2, QT, D])
        h_stats = sb("h_stats", [P, QT, 6])
        h_mv = sb("h_mv", [P, 2, QT, 2])
        h_rstd = sb("h_rstd", [P, 2, QT])
        h_carrier = sb("h_carrier", [P, 1])
        h_eps = sb("h_eps", [P, QT])
        h_half = sb("h_half", [P, QT])
        act_sh = sb("act_sh", [P, 2, SQ])
        gated = sb("gated", [P, 2, SQ])
        logits = sb("logits", [P, NT, E])
        tri = sb("tri", [P, P])
        all_ones = sb("all_ones", [P, P])
        e_iota = sb("e_iota", [P, E])
        t_iota = sb("t_iota", [1, TILES])
        ex = sb("ex", [P, NT, E])
        eq = sb("eq", [P, NT, E])
        left = sb("left", [P, NT, E])
        z_sum = sb("z_sum", [P, NT])
        e2 = sb("e2", [P, NT])
        den = sb("den", [P, NT])
        choice = sb("choice", [P, 2, NT])
        best = sb("best", [P, 2, NT])
        w_top = sb("w_top", [P, 2, NT])
        w_id = sb("w_id", [P, 3, NT])
        hot = sb("hot", [P, 3, NT, E])
        scan = sb("scan", [P, 2, NT, E])
        count = sb("count", [P, 4, E])
        count_i = sb("count_i", [P, E], I32)
        slot = sb("slot", [P, NT, E])
        slot_f = sb("slot_f", [P, 2, NT])
        slot_i = sb("slot_i", [P, 2, NT], U32)
        ge = sb("ge", [1, TILES, E])
        tile_f = sb("tile_f", [1, TILES])
        tile_e = sb("tile_e", [1, TILES], I32)
        xs = sb("xs", [P, 4, D])
        xT = sb("xT", [P, 2, D])
        act_e = sb("act_e", [P, 2, I])
        he = sb("he", [P, 2, I])
        heT = sb("heT", [P, 2, I])
        ys = sb("ys", [P, 4, D])
        yg = sb("yg", [P, 4, 2, D])

        pt = banks("pt", 2)
        pg = banks("pg", 2)
        ph = banks("ph", 2)
        py = banks("py", 2)
        tap_bank = [py[0], py[1], ph[0]]

        misc_in = sem("misc_in")
        conv_in = sem("conv_in")
        exp_in = sem("exp_in")
        bconsts = sem("bconsts")
        btables = sem("btables")
        h_var = sem("h_var")
        h_std = sem("h_std")
        hid_ready = sem("hid_ready")
        hid_kept = sem("hid_kept")
        cv_full = sem("cv_full")
        cv_ready = sem("cv_ready")
        t_full = sem("t_full")
        hT_ready = sem("hT_ready")
        rows_back = sem("rows_back")
        t2_full = sem("t2_full")
        hT2_ready = sem("hT2_ready")
        down_full = sem("down_full")
        shared_added = sem("shared_added")
        gu_full = sem("gu_full")
        silu_done = sem("silu_done")
        gated_ready = sem("gated_ready")
        logits_full = sem("logits_full")
        logits_read = sem("logits_read")
        route = sem("route")
        route_exp = sem("route_exp")
        rank_full = sem("rank_full")
        routed = sem("routed")
        scattered = sem("scattered")
        xs_in = [sem(f"xs_in{i}") for i in range(4)]
        xT_full = sem("xT_full")
        xT_ready = sem("xT_ready")
        egu_full = sem("egu_full")
        esilu = sem("esilu")
        he_ready = sem("he_ready")
        heT_full = sem("heT_full")
        heT_ready = sem("heT_ready")
        ey_full = sem("ey_full")
        ey_ready = sem("ey_ready")
        ys_out = [sem(f"ys_out{i}") for i in range(4)]
        yg_in = [sem(f"yg_in{i}") for i in range(4)]
        identity_added = sem("identity_added")
        first_added = sem("first_added")
        h_chain = sem("h_chain")
        route_step = sem("route_step")
        ex_ready = sem("ex_ready")
        final = sem("final")
        stored = sem("stored")

        OFF = 4 * E

        def pipeline(eng, step, tiles, lags, unroll, peeled, tail=0):
            for s_ in range(peeled):
                step(s_, s_ % unroll, [0 <= s_ - n < tiles for n in range(lags)])
            assert (tiles - peeled - tail) % unroll == 0 and peeled % unroll == 0
            with eng.Fori(0, (tiles - peeled - tail) // unroll) as i:
                for u in range(unroll):
                    step(peeled + unroll * i + u, u, [True] * lags)
            for s_ in range(tiles - tail, tiles + lags - 1):
                step(s_, s_ % unroll, [0 <= s_ - n < tiles for n in range(lags)])

        def router_pass(eng, step):
            pipeline(eng, step, B, 2, 2, 4, tail=2)

        def shared_pass(eng, step):
            pipeline(eng, step, B, 3, 2, 4, tail=2)

        def routed_tiles(eng, step):
            pipeline(eng, step, TILES, 4, 4, 8)

        def known(v):
            return not isinstance(v, int) or v >= 1

        def rows_of(t, bt):
            return t[:, bass.ds(bt, 1), :].rearrange("p a d -> p (a d)")

        block = c.enter_context(nc.Block())

        @block.sync
        def _(sp):
            sp.dma_start(conv_raw[:], conv_w).then_inc(conv_in, 16)
            sp.dma_start(w_su[:], sh_up.rearrange("(k p) i -> p k i", p=P)).then_inc(misc_in, 16)
            sp.dma_start(w_sd[:], sh_down).then_inc(misc_in, 16)
            sp.dma_start(w_rt[:], router_w.rearrange("(k p) e -> p k e", p=P)).then_inc(misc_in, 16)
            sp.dma_start(bias[:], router_bias.partition_broadcast(P)).then_inc(misc_in, 16)
            for k in range(KD):
                rows = slice(k * P, (k + 1) * P)
                sp.dma_start(w_gu[:, :, k, 0, :], gate_w[:, rows, :].rearrange("e p i -> p e i")).then_inc(exp_in, 16)
                sp.dma_start(w_gu[:, :, k, 1, :], up_w[:, rows, :].rearrange("e p i -> p e i")).then_inc(exp_in, 16)
            sp.dma_start(w_dn[:], down_w.rearrange("e i d -> i e d")).then_inc(exp_in, 16)
            sp.wait_ge(scattered, 16 * 2 * NT)

            def load(i, u):
                sp.dma_start(xs[:, u], slots_x[bass.ds(i * P, P), :]).then_inc(xs_in[u], 16)

            for i in range(4):
                load(i, i)
            with sp.Fori(0, TILES // 4 - 1) as q:
                for u in range(4):
                    sp.wait_ge(xT_full, 4 * q + u + 1)
                    load(4 * q + u + 4, u)
            for t in range(NT):
                sp.wait_ge(final, t + 1)
                sp.dma_start(out.rearrange("b (q p) d -> p (b q) d", p=P)[:, t, :], X[:, t, :]).then_inc(stored, 16)
            sp.wait_ge(stored, 16 * NT)

        @block.gpsimd
        def _(pool):
            pool.memset(tri[:], 1.0).then_inc(bconsts, 1)
            pool.memset(all_ones[:], 1.0).then_inc(bconsts, 1)
            pool.memset(h_eps[:], EPS).then_inc(bconsts, 1)
            pool.memset(h_half[:], -0.5).then_inc(bconsts, 1)
            pool.memset(hT[:].rearrange("p a k t -> p (a k) t")[:, :, 0:PAD], 0.0).then_inc(bconsts, 1)
            pool.iota(e_iota[:], [[1, E]], base=-OFF, channel_multiplier=0,
                      allow_small_or_imprecise_dtypes=True).then_inc(bconsts, 1)
            pool.iota(t_iota[:], [[P, TILES]], base=0, channel_multiplier=0,
                      allow_small_or_imprecise_dtypes=True).then_inc(bconsts, 1)
            pool.wait_ge(bconsts, 7)
            pool.affine_select(out=tri[:], in_=tri[:], compare_op=ALU.is_gt, fill=0.0, base=0,
                               pattern=[[1, P]], channel_multiplier=-1).then_inc(btables, 1)
            with pool.Fori(0, B // 2) as q:
                for u in range(2):
                    b = 2 * q + u
                    pool.wait_ge(h_var, b + 1)
                    pool.tensor_tensor(h_rstd[:, u, :], h_mv[:, u, :, 1], h_eps[:], ALU.add).then_inc(h_std, 1)
                    pool.wait_ge(h_std, 2 * b + 1)
                    pool.tensor_tensor(h_rstd[:, u, :], h_rstd[:, u, :], h_half[:], ALU.pow).then_inc(h_std, 1)
            pool.wait_ge(hid_kept, B)
            pool.wait_ge(routed, 1)
            for t in range(NT):
                for i in range(2):
                    pool.indirect_dma_start(
                        out=slots_x, out_offset=bass.IndirectOffsetOnAxis(ap=slot_i[:, i, t:t + 1], axis=0),
                        in_=hid[:, t, :], in_offset=None).then_inc(scattered, 16)
            for u in range(4):
                pool.wait_ge(ys_out[u], 16 * (TILES // 4))
            for t in range(NT):
                if t >= 4:
                    pool.wait_ge(final, t - 3)
                for i in range(2):
                    pool.indirect_dma_start(
                        out=yg[:, t % 4, i, :], out_offset=None, in_=slots_y,
                        in_offset=bass.IndirectOffsetOnAxis(ap=slot_i[:, i, t:t + 1], axis=0)
                        ).then_inc(yg_in[t % 4], 16)

        @block.scalar
        def _(act):
            def router_step(s_, u, live):
                if live[0]:
                    act.wait_ge(hid_ready, s_ + 1)
                    nc.scalar.activation(hid[:, bass.ds(QT * s_, QT), :], h_row[:, u], ACT.Copy).then_inc(hid_kept, 1)
                    act.wait_ge(t_full, s_ + 1)
                    if known(s_ - 1):
                        act.wait_ge(logits_full, s_ - 1)
                    nc.scalar.activation(hT[:, u, :, PAD:PAD + SQ],
                                         pt[u][:].rearrange("p (k t) -> p k t", k=KD), ACT.Copy).then_inc(hT_ready, 1)

            router_pass(act, router_step)

            def rows_again(b, u):
                nc.scalar.activation(h_row[:, u], hid[:, bass.ds(QT * b, QT), :], ACT.Copy).then_inc(rows_back, 1)

            act.wait_ge(hid_kept, B)
            act.wait_ge(logits_full, B)
            rows_again(0, 0)

            def shared_step(s_, u, live):
                if live[0]:
                    act.wait_ge(t2_full, s_ + 1)
                    if known(s_ - 1):
                        act.wait_ge(gu_full, s_ - 1)
                    nc.scalar.activation(hT[:, u, :, PAD:PAD + SQ],
                                         pt[u][:].rearrange("p (k t) -> p k t", k=KD), ACT.Copy).then_inc(hT2_ready, 1)
                    if not isinstance(s_, int) or s_ + 1 < B:
                        rows_again(s_ + 1, (u + 1) % 2)
                if live[1]:
                    v = (u - 1) % 2
                    act.wait_ge(gu_full, s_)
                    if known(s_ - 2):
                        act.wait_ge(gated_ready, s_ - 2)
                    nc.scalar.activation(act_sh[:, v, :], pg[v][:, 0:SQ], ACT.Silu).then_inc(silu_done, 1)

            shared_pass(act, shared_step)

            def step(s_, u, live):
                if live[1]:
                    v = (u - 1) % 2
                    act.wait_ge(egu_full, s_)
                    if known(s_ - 2):
                        act.wait_ge(he_ready, s_ - 2)
                    nc.scalar.activation(act_e[:, v, :], pg[v][:, 0:I], ACT.Silu).then_inc(esilu, 1)
                if live[2]:
                    v = u % 2
                    act.wait_ge(heT_full, s_ - 1)
                    if known(s_ - 3):
                        act.wait_ge(ey_full, s_ - 3)
                    nc.scalar.activation(heT[:, v, :], ph[v][:, 0:I], ACT.Copy).then_inc(heT_ready, 1)
                if live[3]:
                    r = (u - 3) % 4
                    act.wait_ge(ey_ready, s_ - 2)
                    act.dma_start(slots_y[bass.ds((s_ - 3) * P, P), :], ys[:, r, :]).then_inc(ys_out[r], 16)

            routed_tiles(act, step)
            act.wait_ge(ex_ready, 1)
            nc.scalar.activation(ex[:], ex[:], ACT.Exp).then_inc(route_exp, 1)
            nc.scalar.activation(e2[:], e2[:], ACT.Exp).then_inc(route_exp, 1)

        @block.vector
        def _(dve):
            tt, ts = nc.vector.tensor_tensor, nc.vector.tensor_scalar

            def rows_stats(b, u):
                for t in range(QT):
                    last = nc.vector.bn_stats(h_stats[:, t, :], rows_of(X, QT * b + t))
                last.then_inc(h_chain, 1)
                dve.wait_ge(h_chain, b + 1)
                nc.vector.memset(h_carrier[:], 0.0)
                for t in range(QT):
                    last = nc.vector.bn_aggr(h_mv[:, u, t, :], h_stats[:, t, :])
                last.then_inc(h_var, 1)

            dve.wait_ge(bconsts, 7)
            rows_stats(0, 0)
            for j in range(KS_):
                dve.wait_ge(cv_full, j + 1)
                nc.vector.tensor_copy(w_cv[:, j, :, :],
                                      tap_bank[j][:, 0:KD * I].rearrange("p (k i) -> p k i", k=KD)
                                      ).then_inc(cv_ready, 1)
            dve.wait_ge(misc_in, 16 * 4)

            def router_step(s_, u, live):
                if live[0]:
                    if known(s_ - 1):
                        dve.wait_ge(hid_kept, s_ - 1)
                        dve.wait_ge(t_full, s_ - 1)
                    dve.wait_ge(h_std, 2 * s_ + 2)
                    for t in range(QT):
                        last = ts(h_row[:, u, t, :], rows_of(X, QT * s_ + t),
                                  h_mv[:, u, t, 0:1], h_rstd[:, u, t:t + 1], ALU.subtract, ALU.mult)
                    last.then_inc(hid_ready, 1)
                    if not isinstance(s_, int) or s_ + 1 < B:
                        rows_stats(s_ + 1, (u + 1) % 2)
                if live[1]:
                    v = (u - 1) % 2
                    dve.wait_ge(logits_full, s_)
                    tt(logits[:, bass.ds(QT * (s_ - 1), QT), :],
                       ph[v][:, 0:QT * E].rearrange("p (t e) -> p t e", t=QT),
                       bias[:].unsqueeze(1).to_broadcast([P, QT, E]), ALU.add).then_inc(logits_read, 1)

            router_pass(dve, router_step)

            steps = [0]

            def then(ins):
                steps[0] += 1
                ins.then_inc(route_step, 1)
                dve.wait_ge(route_step, steps[0])

            def over_e(v):
                return v.unsqueeze(2).to_broadcast([P, NT, E])

            def over_t(v):
                return v.unsqueeze(1).to_broadcast([P, NT, E])

            dve.wait_ge(logits_read, B)
            dve.wait_ge(hid_kept, B)
            for i in range(2):
                src = logits if i == 0 else left
                then(nc.vector.tensor_reduce(best[:, i, :], src[:], AX.X, ALU.max))
                then(tt(eq[:], src[:], over_e(best[:, i, :]), ALU.is_equal))
                then(tt(eq[:], eq[:], over_t(e_iota[:]), ALU.mult))
                then(nc.vector.tensor_reduce(choice[:, i, :], eq[:], AX.X, ALU.min))
                then(tt(hot[:, i], over_t(e_iota[:]), over_e(choice[:, i, :]), ALU.is_equal))
                if i == 0:
                    then(nc.vector.scalar_tensor_tensor(left[:], hot[:, 0], -1e38, logits[:], ALU.mult, ALU.add))
            tt(hot[:, 2], hot[:, 0], hot[:, 1], ALU.add).then_inc(route, 1)
            in_tile = py[0][:].rearrange("p (t e) -> p t e", e=E)
            of_tile = py[1][:].rearrange("p (t e) -> p t e", e=E)
            dve.wait_ge(rank_full, 1)
            then(nc.vector.tensor_copy(scan[:, 0], of_tile))
            cur, d = 0, 1
            while d < NT:
                nc.vector.tensor_copy(scan[:, 1 - cur, 0:d, :], scan[:, cur, 0:d, :])
                then(tt(scan[:, 1 - cur, d:NT, :], scan[:, cur, d:NT, :], scan[:, cur, 0:NT - d, :], ALU.add))
                cur, d = 1 - cur, 2 * d
            total = scan[:, cur, NT - 1, :]
            shift = P.bit_length() - 1
            then(ts(count_i[:], total, float(P - 1), None, ALU.add))
            then(ts(count_i[:], count_i[:], shift, shift, ALU.logical_shift_right, ALU.logical_shift_left))
            nc.vector.tensor_copy(count[:, 0, :], count_i[:])
            then(nc.vector.tensor_copy(count[:, 1, :], count_i[:]))
            a, b_, d = 1, 2, 1
            while d < E:
                nc.vector.tensor_copy(count[:, b_, 0:d], count[:, a, 0:d])
                then(tt(count[:, b_, d:E], count[:, a, d:E], count[:, a, 0:E - d], ALU.add))
                a, b_, d = b_, a, 2 * d
            ends = count[:, a, :]
            then(tt(count[:, 3, :], ends, count[:, 0, :], ALU.subtract))
            then(tt(ge[:], count[0:1, a, :].unsqueeze(1).to_broadcast([1, TILES, E]),
                    t_iota[:].unsqueeze(2).to_broadcast([1, TILES, E]), ALU.is_le))
            then(nc.vector.tensor_reduce(tile_f[:], ge[:], AX.X, ALU.add))
            then(ts(tile_e[:], tile_f[:], float(NE - 1), None, ALU.min))
            then(tt(slot[:], in_tile, scan[:, cur], ALU.add))
            then(tt(slot[:], slot[:], over_t(count[:, 3, :]), ALU.add))
            then(tt(slot[:], of_tile, slot[:], ALU.subtract))
            for i in range(2):
                then(tt(eq[:], hot[:, i], slot[:], ALU.mult))
                then(nc.vector.tensor_reduce(slot_f[:, i, :], eq[:], AX.X, ALU.add))
            ts(slot_i[:], slot_f[:], -1.0, None, ALU.mult).then_inc(routed, 1)

            def shared_step(s_, u, live):
                if live[1]:
                    v = (u - 1) % 2
                    dve.wait_ge(silu_done, s_)
                    if known(s_ - 2):
                        dve.wait_ge(down_full, s_ - 2)
                    tt(gated[:, v, :], pg[v][:, SQ:2 * SQ], act_sh[:, v, :], ALU.mult).then_inc(gated_ready, 1)
                if live[2]:
                    dve.wait_ge(down_full, s_ - 1)
                    for t in range(QT):
                        row = rows_of(X, QT * (s_ - 2) + t)
                        last = nc.vector.scalar_tensor_tensor(row, py[u][:, t * D:(t + 1) * D], tanh_g[:, 1:2], row,
                                                              ALU.mult, ALU.add)
                    last.then_inc(shared_added, 1)

            shared_pass(dve, shared_step)

            def step(s_, u, live):
                if live[0]:
                    v = u % 2
                    dve.wait_ge(xT_full, s_ + 1)
                    if known(s_ - 1):
                        dve.wait_ge(egu_full, s_ - 1)
                    nc.vector.tensor_copy(xT[:, v, :], pt[v][:, 0:D]).then_inc(xT_ready, 1)
                if live[1]:
                    v = (u - 1) % 2
                    dve.wait_ge(esilu, s_)
                    if known(s_ - 2):
                        dve.wait_ge(heT_full, s_ - 2)
                    tt(he[:, v, :], pg[v][:, I:2 * I], act_e[:, v, :], ALU.mult).then_inc(he_ready, 1)
                if live[3]:
                    v, r = (u - 3) % 2, (u - 3) % 4
                    dve.wait_ge(ey_full, s_ - 2)
                    turns = 16 * ((s_ - 3) // 4) if isinstance(s_, int) else 4 * (s_ - u - (0 if u == 3 else 4))
                    if known(turns):
                        dve.wait_ge(ys_out[r], turns)
                    nc.vector.tensor_copy(ys[:, r, :], py[v][:, 0:D]).then_inc(ey_ready, 1)

            routed_tiles(dve, step)

            tt(e2[:], best[:, 1, :], best[:, 0, :], ALU.subtract)
            tt(ex[:], logits[:], over_e(best[:, 0, :]), ALU.subtract).then_inc(ex_ready, 1)
            dve.wait_ge(route_exp, 2)
            then(nc.vector.tensor_reduce(z_sum[:], ex[:], AX.X, ALU.add))
            then(nc.vector.scalar_tensor_tensor(den[:], z_sum[:], 1e-6, e2[:], ALU.mult, ALU.add))
            then(ts(den[:], den[:], 1.0, None, ALU.add))
            then(nc.vector.reciprocal(w_top[:, 0, :], den[:]))
            then(ts(w_top[:, 0, :], w_top[:, 0, :], tanh_g[:, 1:2], None, ALU.mult))
            then(tt(w_top[:, 1, :], w_top[:, 0, :], e2[:], ALU.mult))
            then(ts(w_id[:, 0:2, :], choice[:], float(E - 1 - OFF), None, ALU.is_equal))
            then(tt(w_id[:, 0:2, :], w_id[:, 0:2, :], w_top[:], ALU.mult))
            tt(w_top[:], w_top[:], w_id[:, 0:2, :], ALU.subtract)
            then(tt(w_id[:, 2, :], w_id[:, 0, :], w_id[:, 1, :], ALU.add))

            def add(t, i):
                return nc.vector.scalar_tensor_tensor(X[:, t, :], yg[:, t % 4, i, :], w_top[:, i, t:t + 1],
                                                      X[:, t, :], ALU.mult, ALU.add)

            def add_identity(t):
                return nc.vector.scalar_tensor_tensor(X[:, t, :], hid[:, t, :], w_id[:, 2, t:t + 1], X[:, t, :],
                                                      ALU.mult, ALU.add)

            dve.wait_ge(shared_added, B)
            for t in range(NT + 2):
                if t < NT:
                    add_identity(t).then_inc(identity_added, 1)
                if 1 <= t < NT + 1:
                    dve.wait_ge(identity_added, t)
                    dve.wait_ge(yg_in[(t - 1) % 4], 32 * ((t - 1) // 4 + 1))
                    add(t - 1, 0).then_inc(first_added, 1)
                if t >= 2:
                    dve.wait_ge(first_added, t - 1)
                    add(t - 2, 1).then_inc(final, 1)

        @block.tensor
        def _(pe):
            pe.wait_ge(conv_in, 16)
            for j in range(KS_):
                for k in range(KD):
                    last = nc.tensor.transpose(tap_bank[j][:, k * I:(k + 1) * I],
                                               conv_raw[:, k * P:(k + 1) * P, j], ident[:])
                last.then_inc(cv_full, 1)
            pe.wait_ge(misc_in, 16 * 4)
            pe.wait_ge(bconsts, 7)
            pe.wait_ge(btables, 1)
            pe.wait_ge(cv_ready, KS_)

            def transposes(u, full):
                for t in range(QT):
                    for k in range(KD):
                        last = nc.tensor.transpose(pt[u][:, k * SQ + t * P:k * SQ + (t + 1) * P],
                                                   h_row[:, u, t, k * P:(k + 1) * P], ident[:])
                last.then_inc(full, 1)

            def router_step(s_, u, live):
                if live[0]:
                    pe.wait_ge(hid_ready, s_ + 1)
                    if known(s_ - 1):
                        pe.wait_ge(hT_ready, s_ - 1)
                    transposes(u, t_full)
                if live[1]:
                    v = (u - 1) % 2
                    pe.wait_ge(hT_ready, s_)
                    if known(s_ - 2):
                        pe.wait_ge(logits_read, s_ - 2)
                    for t in range(QT):
                        for k in range(KD):
                            last = nc.tensor.matmul(ph[v][:, t * E:(t + 1) * E],
                                                    hT[:, v, k, PAD + t * P:PAD + (t + 1) * P], w_rt[:, k, :],
                                                    start=(k == 0), stop=(k == KD - 1))
                    last.then_inc(logits_full, 1)

            router_pass(pe, router_step)

            def shared_step(s_, u, live):
                if live[0]:
                    pe.wait_ge(rows_back, s_ + 1)
                    if known(s_ - 1):
                        pe.wait_ge(hT2_ready, s_ - 1)
                    transposes(u, t2_full)
                if live[1]:
                    v = (u - 1) % 2
                    pe.wait_ge(hT2_ready, s_)
                    if known(s_ - 2):
                        pe.wait_ge(gated_ready, s_ - 2)
                    taps = [(k, j) for k in range(KD) for j in range(KS_)]
                    for n, (k, j) in enumerate(taps):
                        nc.tensor.matmul(pg[v][:, 0:SQ], w_cv[:, j, k, :], hT[:, v, k, j:j + SQ],
                                         start=(n == 0), stop=(n == len(taps) - 1))
                    for k in range(KD):
                        last = nc.tensor.matmul(pg[v][:, SQ:2 * SQ], w_su[:, k, :], hT[:, v, k, PAD:PAD + SQ],
                                                start=(k == 0), stop=(k == KD - 1))
                    last.then_inc(gu_full, 1)
                if isinstance(s_, int) and s_ == 1:
                    pe.wait_ge(route, 1)
                    flat = hot[:, 2].rearrange("p t e -> p (t e)")
                    nc.tensor.matmul(py[0][:], tri[:], flat, start=True, stop=True)
                    nc.tensor.matmul(py[1][:], all_ones[:], flat, start=True, stop=True).then_inc(rank_full, 1)
                if live[2]:
                    pe.wait_ge(gated_ready, s_ - 1)
                    if known(s_ - 3):
                        pe.wait_ge(shared_added, s_ - 3)
                    for t in range(QT):
                        last = nc.tensor.matmul(py[u][:, t * D:(t + 1) * D], gated[:, u, t * P:(t + 1) * P], w_sd[:],
                                                start=True, stop=True)
                    last.then_inc(down_full, 1)

            shared_pass(pe, shared_step)
            pe.wait_ge(routed, 1)
            pe.wait_ge(shared_added, B)
            pe.wait_ge(exp_in, 16 * (2 * KD + 1))

            expert_reg = [pe.alloc_register(f"expert{i}") for i in range(4)]

            def fetch_expert(tile, r):
                pe.reg_load(expert_reg[r], tile_e[0:1, bass.ds(tile, 1)])

            def expert_of(r):
                return pe.snap(expert_reg[r], min_val=0, max_val=NE - 1)

            fetch_expert(0, 0)

            def step(s_, u, live):
                if live[0]:
                    v = u % 2
                    pe.wait_ge(xs_in[u], (16 * (s_ // 4 + 1)) if isinstance(s_, int) else 4 * (s_ - u + 4))
                    if known(s_ - 1):
                        pe.wait_ge(xT_ready, s_ - 1)
                    for k in range(KD):
                        last = nc.tensor.transpose(pt[v][:, k * P:(k + 1) * P], xs[:, u, k * P:(k + 1) * P], ident[:])
                    last.then_inc(xT_full, 1)
                if live[1]:
                    v = (u - 1) % 2
                    e = expert_of((u - 1) % 4)
                    pe.wait_ge(xT_ready, s_)
                    if known(s_ - 2):
                        pe.wait_ge(he_ready, s_ - 2)
                    for k in range(KD):
                        last = nc.tensor.matmul(pg[v][:, 0:2 * I], xT[:, v, k * P:(k + 1) * P],
                                                w_gu[:, bass.ds(e, 1), k].rearrange("p a g i -> p (a g i)"),
                                                start=(k == 0), stop=(k == KD - 1))
                    last.then_inc(egu_full, 1)
                if live[0] and known(s_):
                    fetch_expert(s_, u)
                if live[2]:
                    v = u % 2
                    pe.wait_ge(he_ready, s_ - 1)
                    if known(s_ - 3):
                        pe.wait_ge(heT_ready, s_ - 3)
                    nc.tensor.transpose(ph[v][:, 0:I], he[:, v, :], ident[:]).then_inc(heT_full, 1)
                if live[3]:
                    v = (u - 3) % 2
                    e = expert_of((u - 3) % 4)
                    pe.wait_ge(heT_ready, s_ - 2)
                    if known(s_ - 4):
                        pe.wait_ge(ey_ready, s_ - 4)
                    nc.tensor.matmul(py[v][:, 0:D], heT[:, v, :],
                                     w_dn[:, bass.ds(e, 1), :].rearrange("p a d -> p (a d)"),
                                     start=True, stop=True).then_inc(ey_full, 1)

            routed_tiles(pe, step)


def attention(nc, X, ident, tanh_g, x, ctx_in, g_xattn, g_ffn, ln1_g, ln1_b, ln2_g, ln2_b,
              Wq, Wkv, Wo, slots_x, s):
    B, SQ, D, SC, INNER, DH, H, PAIRS, KD, QT, SKV, SKVE, KT, NKT, EPS, SCALE = (
        s[n] for n in "B SQ D SC INNER DH H PAIRS KD QT SKV SKVE KT NKT EPS SCALE".split())
    N = B * PAIRS
    UNROLL = 2 * PAIRS
    LAG_APX, LAG_ROW, LAG_S, LAG_AV, LAG_NORM, LAG_Y = 1, 2, 3, 4, 4, 5
    RING = 4
    V_STEPS = {0: 0, 1: 1, 2: 2, 4: 3, 5: 4, 6: 5}
    L_STEPS = {3: 0, 4: 1}

    with ExitStack() as c:
        def sb(name, shape, dt=F32):
            return c.enter_context(nc.sbuf_tensor(name, shape, dt))

        def sem(name):
            return c.enter_context(nc.semaphore(name))

        def banks(name, n):
            return [c.enter_context(nc.psum_tensor(f"{name}{i}", [P, 512], F32)) for i in range(n)]

        wq = sb("wq", [P, 2, KD, INNER], F32R)
        wkv = sb("wkv", [P, 2, KD, 2 * INNER], F32R)
        wo = sb("wo", [P, PAIRS, D])
        stage = sb("stage", [P, 2, INNER])
        gb = sb("gb", [P, 4, KD])
        ones = sb("ones", [P, DH])
        neg_half = sb("neg_half", [P, 4])
        eps = sb("eps", [P, 4])
        carrier = sb("carrier", [P, 1])
        zeros = sb("zeros", [P, D])
        ctx_t = sb("ctx_t", [P, D])
        z = sb("z", [P, QT + 1, D])
        stats = sb("stats", [P, QT + 1, 6])
        mv = sb("mv", [P, 2, QT + 1, 2])
        rstd = sb("rstd", [P, 2, QT + 1])
        lT32 = sb("lT32", [P, KD, SKVE])
        lT = sb("lT", [P, 2, 2, KD, SKVE], F32R)
        KS = sb("KS", [P, RING, 2, 2, SKVE], F32R)
        QS = sb("QS", [P, RING, 2, 2, SQ], F32R)
        V = sb("V", [P, NKT, INNER])
        neg_max = sb("neg_max", [P, 2, 2, QT])
        probs = sb("probs", [P, 2, NKT, 2 * SQ])
        prob_sum = sb("prob_sum", [P, 2, 2 * SQ])
        inv_sum = sb("inv_sum", [P, 2, SQ])
        OT = sb("OT", [P, 2, SQ])

        pj = banks("pj", 2)
        st = banks("st", 4)
        ov = banks("ov", 1)[0]
        yb = banks("yb", 1)[0]

        x_in = sem("x_in")
        ctx_loaded = sem("ctx_loaded")
        ctx_used = sem("ctx_used")
        ln_in = sem("ln_in")
        gate_in = sem("gate_in")
        w_in = [sem("w_in0"), sem("w_in1")]
        wo_in = sem("wo_in")
        w_hi = sem("w_hi")
        w_lo = sem("w_lo")
        consts = sem("consts")
        tables = sem("tables")
        one_rows = sem("one_rows")
        gates = sem("gates")
        zeros_set = sem("zeros_set")
        slots_clear = sem("slots_clear")
        ln_dve = sem("ln_dve")
        ln_rstd = sem("ln_rstd")
        ln_chain = sem("ln_chain")
        rows_ready = sem("rows_ready")
        lt_ready = sem("lt_ready")
        pj_full = sem("pj_full")
        pj_free = [sem(f"pj_free{i}") for i in range(len(pj))]
        q_hi = sem("q_hi")
        k_hi = sem("k_hi")
        q_dup = [sem(f"q_dup{i}") for i in range(RING)]
        st_full = sem("st_full")
        st_free = [sem(f"st_free{i}") for i in range(len(st))]
        summed = sem("summed")
        ov_full = sem("ov_full")
        inv_ready = sem("inv_ready")
        ot_ready = sem("ot_ready")
        y_full = sem("y_full")
        y_read = sem("y_read")

        def fills(n):
            b, p = divmod(n, PAIRS)
            order = []

            def lagged(lag, ring, kind, per, i):
                if 0 <= n - lag < N:
                    order.append((ring, kind, per * (n - lag) + i))

            lagged(0, 0, "Q", 1, 0)
            lagged(LAG_S, 1, "S", NKT, 0)
            lagged(0, 0, "K", 1, 0)
            lagged(LAG_S, 1, "S", NKT, 1)
            lagged(LAG_S, 1, "S", NKT, 2)
            for i in range(4):
                lagged(LAG_APX, 1, "A", 4, i)
            if p in V_STEPS and b < B:
                order.append((0, "V", len(V_STEPS) * b + V_STEPS[p]))
            lagged(LAG_ROW, 0, "M", 1, 0)
            if p in L_STEPS and b + 1 < B:
                order.append((0, "L", KD * (b + 1) + L_STEPS[p]))
            return order

        number, rings = {}, (pj, st)
        totals = [KD, 0]
        for k in range(KD):
            number["L", k] = k
        in_loop = [0, 0]
        for n in range(N + LAG_Y):
            for ring, kind, i in fills(n):
                number[kind, i] = totals[ring]
                totals[ring] += 1
                in_loop[ring] += UNROLL <= n < 2 * UNROLL
        frees = (pj_free, st_free)
        assert all(f % (2 * len(r)) == 0 for f, r in zip(in_loop, rings))

        def filled(kind, per, bb, off):
            ring = 0 if kind in "QKVML" else 1
            size, a_batch = len(rings[ring]), in_loop[ring] // 2
            if isinstance(bb, int):
                n = number[kind, per * bb + off]
                return n, rings[ring][n % size], frees[ring][n % size], n // size + 1
            n = number[kind, 2 * per + off]
            assert number[kind, 4 * per + off] == n + 2 * a_batch
            return (a_batch * (bb - 2) + n, rings[ring][n % size], frees[ring][n % size],
                    a_batch // size * (bb - 2) + (n // size + 1))

        def pipeline(eng, step):
            def written_out(n):
                bb = n // UNROLL * 2
                step(bb, n - PAIRS * bb, lambda lag: 0 <= n - lag < N)

            for n in range(UNROLL):
                written_out(n)
            with eng.Fori(0, (N - 2 * UNROLL) // UNROLL) as i:
                for u in range(UNROLL):
                    step(2 * i + 2, u, lambda lag: True)
            for n in range(N - UNROLL, N + LAG_Y + 1):
                written_out(n)

        def exists(b):
            return not isinstance(b, int) or b < B

        def known(v):
            return not isinstance(v, int) or v >= 1

        block = c.enter_context(nc.Block())

        @block.sync
        def _(sp):
            sp.dma_start(ctx_t[0:SC, :], ctx_in[0]).then_inc(ctx_loaded, 16)
            sp.dma_start(X[:], x.rearrange("b (q p) d -> p (b q) d", p=P)).then_inc(x_in, 16)
            for i, v in enumerate((ln1_g, ln1_b, ln2_g, ln2_b)):
                sp.dma_start(gb[:, i, :], v.rearrange("(k p) -> p k", p=P),
                             allow_slow_non_contiguous=True).then_inc(ln_in, 16)
            pieces = [(Wq, k, 0) for k in range(KD)] + [(Wkv, k, n) for n in range(2) for k in range(KD)]
            for i, (w, k, n) in enumerate(pieces):
                if i >= 2:
                    sp.wait_ge(w_lo, i - 1)
                sp.dma_start(stage[:, i % 2, :], w[k * P:(k + 1) * P, n * INNER:(n + 1) * INNER]
                             ).then_inc(w_in[i % 2], 16)
            sp.dma_start(wo[:], Wo.rearrange("(q p) d -> p q d", p=P)).then_inc(wo_in, 16)
            sp.wait_ge(zeros_set, 1)
            tiles = slots_x.shape[0] // P
            sp.dma_start(slots_x.rearrange("(t p) d -> p t d", p=P),
                         zeros[:].unsqueeze(1).to_broadcast([P, tiles, D])).then_inc(slots_clear, 16)

            def step(bb, u, has):
                r = u % RING
                if has(0):
                    sp.wait_ge(q_hi, PAIRS * bb + u + 1)
                    sp.dma_start(QS[HALF:P, r, 0, 0].bitcast(F32), QS[0:HALF, r, 0, 0].bitcast(F32)
                                 ).then_inc(q_dup[r], 16)
                    sp.dma_start(QS[0:HALF, r, 1, 0].bitcast(F32), QS[HALF:P, r, 1, 0].bitcast(F32)
                                 ).then_inc(q_dup[r], 16)
                b = bb + u // PAIRS
                if u % PAIRS == 6 and exists(b + 2):
                    sp.wait_ge(ctx_used, b + 2)
                    sp.dma_start(ctx_t[0:SC, :], ctx_in[bass.ds(b + 2, 1)].rearrange("a s d -> (a s) d")
                                 ).then_inc(ctx_loaded, 16)

            sp.wait_ge(ctx_used, 1)
            sp.dma_start(ctx_t[0:SC, :], ctx_in[1]).then_inc(ctx_loaded, 16)
            pipeline(sp, step)
            sp.wait_ge(slots_clear, 16)

        @block.gpsimd
        def _(pool):
            pool.memset(ident[:], 0.0).then_inc(consts, 1)
            pool.memset(ones[:], 1.0).then_inc(consts, 1)
            pool.memset(neg_half[:], -0.5).then_inc(consts, 1)
            pool.memset(eps[:], EPS).then_inc(consts, 1)
            pool.memset(mv[:].rearrange("p a t s -> p (a t s)"), 1.0).then_inc(consts, 1)
            pool.memset(lT32[:, :, SKV:SKVE], 0.0).then_inc(consts, 1)
            pool.wait_ge(consts, 1)
            pool.affine_select(out=ident[:], in_=ident[:], compare_op=ALU.not_equal, fill=1.0, base=0,
                               pattern=[[-1, P]], channel_multiplier=1).then_inc(tables, 1)
            pool.memset(zeros[:], 0.0).then_inc(zeros_set, 1)
            pool.wait_ge(consts, 6)

            def inv_std(j, which, n):
                pool.wait_ge(ln_dve, 2 * j + 1 + which)
                pool.tensor_tensor(rstd[:, which, 0:n], mv[:, which, 0:n, 1], eps[:, 0:n], ALU.add
                                   ).then_inc(ln_rstd, 1)
                pool.wait_ge(ln_rstd, 4 * j + 2 * which + 1)
                pool.tensor_tensor(rstd[:, which, 0:n], rstd[:, which, 0:n], neg_half[:, 0:n], ALU.pow
                                   ).then_inc(ln_rstd, 1)

            def step(bb, u, has):
                b, p = bb + u // PAIRS, u % PAIRS
                if has(LAG_AV):
                    m, v = PAIRS * bb + u - LAG_AV, (u - LAG_AV) % 2
                    for i in range(NKT):
                        _, _, free, value = filled("S", NKT * PAIRS, bb, NKT * (u - LAG_AV) + i)
                        pool.wait_ge(free, value + 1)
                    if known(m - 1):
                        pool.wait_ge(ov_full, m - 1)
                    total = prob_sum[:, v, :].rearrange("p (h q) -> p h q", h=2)
                    pool.tensor_tensor(total, probs[:, v, 0:2, 0:SQ], probs[:, v, 0:2, SQ:2 * SQ], ALU.add
                                       ).then_inc(summed, 1)
                    pool.wait_ge(summed, 2 * m + 1)
                    kn = KT[2][1]
                    pool.tensor_tensor(prob_sum[0:kn, v, :], prob_sum[0:kn, v, :], probs[0:kn, v, 2, :], ALU.add
                                       ).then_inc(summed, 1)
                if p < 2 and exists(b + 1) and exists(b):
                    inv_std(b + 1, p, QT + 1 - p)

            inv_std(0, 0, QT + 1)
            inv_std(0, 1, QT)
            pipeline(pool, step)

        @block.scalar
        def _(act):
            act.dma_start(tanh_g[:, 0:1], g_xattn.partition_broadcast(P)).then_inc(gate_in, 16)
            act.dma_start(tanh_g[:, 1:2], g_ffn.partition_broadcast(P)).then_inc(gate_in, 16)
            hi = [wq[:, 0, k, :] for k in range(KD)] + \
                 [wkv[:, 0, k, n * INNER:(n + 1) * INNER] for n in range(2) for k in range(KD)]
            for i, w in enumerate(hi):
                act.wait_ge(w_in[i % 2], 16 * (i // 2 + 1))
                nc.scalar.activation(w, stage[:, i % 2, :], ACT.Copy).then_inc(w_hi, 1)
            act.wait_ge(gate_in, 32)
            nc.scalar.activation(tanh_g[:], tanh_g[:], ACT.Tanh).then_inc(gates, 1)
            act.wait_ge(one_rows, 1)

            def step(bb, u, has):
                b, p, r = bb + u // PAIRS, u % PAIRS, u % RING
                copy = nc.scalar.activation

                def exp(i):
                    v = (u - LAG_S) % 2
                    n, bank, free, _ = filled("S", NKT * PAIRS, bb, NKT * (u - LAG_S) + i)
                    m = PAIRS * bb + u - LAG_S
                    if i == 0 and known(m - 1):
                        act.wait_ge(ov_full, m - 1)
                    kn = KT[2][1] if i == 2 else P
                    act.wait_ge(st_full, n + 1)
                    nc.scalar.activation(probs[0:kn, v, i, :], bank[0:kn, :], ACT.Exp, scale=SCALE).then_inc(free, 1)

                if has(0):
                    n, bank, _, _ = filled("Q", PAIRS, bb, u)
                    act.wait_ge(pj_full, n + 1)
                    copy(QS[0:HALF, r, 0, 0, :], bank[0:HALF, 0:SQ], ACT.Copy)
                    copy(QS[HALF:P, r, 1, 0, :], bank[HALF:P, 0:SQ], ACT.Copy).then_inc(q_hi, 1)
                if has(LAG_S):
                    exp(0)
                if has(0):
                    n, bank, _, _ = filled("K", PAIRS, bb, u)
                    act.wait_ge(pj_full, n + 1)
                    for half in range(2):
                        rows = slice(half * HALF, (half + 1) * HALF)
                        last = copy(KS[rows, r, half, :, :],
                                    bank[rows, 0:SKVE].unsqueeze(1).to_broadcast([HALF, 2, SKVE]), ACT.Copy)
                    last.then_inc(k_hi, 1)
                if has(LAG_S):
                    exp(1)
                    exp(2)
                if p in V_STEPS and has(0):
                    kt, half = V_STEPS[p] % NKT, V_STEPS[p] // NKT
                    kn = KT[kt][1]
                    n, bank, free, _ = filled("V", len(V_STEPS), bb, len(V_STEPS) * (u // PAIRS) + V_STEPS[p])
                    act.wait_ge(pj_full, n + 1)
                    copy(V[0:kn, kt, half * 512:(half + 1) * 512], bank[0:kn, :], ACT.Copy).then_inc(free, 1)
                if has(LAG_ROW):
                    n, bank, free, _ = filled("M", PAIRS, bb, u - LAG_ROW)
                    r = (u - LAG_ROW) % RING
                    act.wait_ge(pj_full, n + 1)
                    copy(QS[HALF:HALF + 2, r, 0, 1, :], bank[0:2, 0:SQ], ACT.Copy)
                    copy(QS[0:2, r, 1, 1, :], bank[0:2, 0:SQ], ACT.Copy).then_inc(free, 1)

            pipeline(act, step)

        @block.vector
        def _(dve):
            tt = nc.vector.tensor_tensor
            for bank in pj_free + st_free:
                dve.sem_inc(bank, 1)
            nc.vector.memset(QS[:, :, :, 1, :].bitcast(F32), 0.0)
            nc.vector.memset(KS[:, :, :, 1, :].bitcast(F32), 0.0)
            dve.wait_ge(tables, 1)

            def layer_norm(j, part, v):
                src = [X[:, bass.ds(QT * j + t, 1), :].rearrange("p a d -> p (a d)") for t in range(QT)]
                C = 2 + KD
                if part == 0:
                    dve.wait_ge(ctx_loaded, 16 * (j + 1))
                    for t in range(QT):
                        nc.vector.bn_stats(stats[:, t, :], src[t])
                    nc.vector.bn_stats(stats[0:SC, QT, :], ctx_t[0:SC, :]).then_inc(ln_chain, 1)
                    dve.wait_ge(ln_chain, C * j + 1)
                    nc.vector.memset(carrier[:], 0.0)
                    for t in range(QT):
                        nc.vector.bn_aggr(mv[:, 0, t, :], stats[:, t, :])
                    nc.vector.bn_aggr(mv[0:SC, 0, QT, :], stats[0:SC, QT, :]).then_inc(ln_dve, 1)
                if part == 1:
                    dve.wait_ge(ln_rstd, 4 * j + 2)
                    for t in range(QT):
                        nc.vector.tensor_scalar(z[:, t, :], src[t], mv[:, 0, t, 0:1], rstd[:, 0, t:t + 1],
                                                ALU.subtract, ALU.mult)
                    nc.vector.tensor_scalar(z[0:SC, QT, :], ctx_t[0:SC, :], mv[0:SC, 0, QT, 0:1],
                                            rstd[0:SC, 0, QT:QT + 1], ALU.subtract, ALU.mult).then_inc(ctx_used, 1)
                    dve.wait_ge(ctx_used, j + 1)
                    for t in range(QT):
                        last = nc.vector.bn_stats(stats[:, t, :], z[:, t, :])
                    last.then_inc(ln_chain, 1)
                    dve.wait_ge(ln_chain, C * j + 2)
                    nc.vector.memset(carrier[:], 0.0)
                    for t in range(QT):
                        last = nc.vector.bn_aggr(mv[:, 1, t, :], stats[:, t, :])
                    last.then_inc(ln_dve, 1)
                if part == 2:
                    dve.wait_ge(ln_rstd, 4 * j + 4)
                    for t in range(QT):
                        last = nc.vector.tensor_scalar(z[:, t, :], z[:, t, :], mv[:, 1, t, 0:1],
                                                       rstd[:, 1, t:t + 1], ALU.subtract, ALU.mult)
                    last.then_inc(rows_ready, 1)

            def transposed(bb, j_off, k, v):
                j = bb + j_off
                C = 2 + KD
                n, bank, free, value = filled("L", KD, bb, KD * j_off + k)
                dve.wait_ge(pj_full, n + 1)
                nc.vector.tensor_scalar(lT32[:, k, 0:SQ], bank[:, 0:SQ], gb[:, 2, k:k + 1],
                                        gb[:, 3, k:k + 1], ALU.mult, ALU.add)
                nc.vector.tensor_scalar(lT32[:, k, SQ:SKV], bank[:, SQ:SKV], gb[:, 0, k:k + 1],
                                        gb[:, 1, k:k + 1], ALU.mult, ALU.add).then_inc(free, 1)
                dve.wait_ge(free, value + 1)
                nc.vector.tensor_copy(lT[:, v, 0, k, :], lT32[:, k, :]).then_inc(ln_chain, 1)
                dve.wait_ge(ln_chain, C * j + 3 + k)
                tt(lT[:, v, 1, k, :], lT32[:, k, :], lT[:, v, 0, k, :].bitcast(F32), ALU.subtract).then_inc(lt_ready, 1)

            dve.wait_ge(x_in, 16)
            dve.wait_ge(ln_in, 16 * 4)
            for part in range(3):
                layer_norm(0, part, 0)
            lo = [(wq, k, 0) for k in range(KD)] + [(wkv, k, n) for n in range(2) for k in range(KD)]

            def split_weights(pieces):
                for i in pieces:
                    w, k, n = lo[i]
                    dve.wait_ge(w_hi, i + 1)
                    cols = slice(n * INNER, (n + 1) * INNER)
                    tt(w[:, 1, k, cols], stage[:, i % 2, :], w[:, 0, k, cols].bitcast(F32), ALU.subtract).then_inc(w_lo, 1)

            split_weights(range(2))
            for k in range(KD):
                transposed(0, 0, k, 0)
            split_weights(range(2, 3 * KD))
            nc.vector.tensor_copy(KS[HALF:HALF + 2, :, 0, 1, :],
                                  ident[0:2, 0:1].unsqueeze(2).to_broadcast([2, RING, SKVE]))
            nc.vector.tensor_copy(KS[0:2, :, 1, 1, :],
                                  ident[0:2, 1:2].unsqueeze(2).to_broadcast([2, RING, SKVE])).then_inc(one_rows, 1)
            dve.wait_ge(gates, 1)

            def step(bb, u, has):
                b, p, r = bb + u // PAIRS, u % PAIRS, u % RING
                if has(0):
                    _, bank, free, _ = filled("Q", PAIRS, bb, u)
                    dve.wait_ge(q_hi, PAIRS * bb + u + 1)
                    tt(QS[0:HALF, r, 0, 1, :], bank[0:HALF, 0:SQ], QS[0:HALF, r, 0, 0, :].bitcast(F32), ALU.subtract)
                    tt(QS[HALF:P, r, 1, 1, :], bank[HALF:P, 0:SQ], QS[HALF:P, r, 1, 0, :].bitcast(F32), ALU.subtract
                       ).then_inc(free, 1)
                    _, bank, free, _ = filled("K", PAIRS, bb, u)
                    dve.wait_ge(k_hi, PAIRS * bb + u + 1)
                    tt(KS[HALF:P, r, 0, 0, :], bank[0:HALF, 0:SKVE], KS[0:HALF, r, 0, 0, :].bitcast(F32), ALU.subtract)
                    tt(KS[0:HALF, r, 1, 0, :], bank[HALF:P, 0:SKVE], KS[HALF:P, r, 1, 0, :].bitcast(F32), ALU.subtract
                       ).then_inc(free, 1)
                if exists(b + 1) and exists(b) and p < 3:
                    layer_norm(b + 1, p, 0)
                if has(LAG_NORM):
                    m, v = PAIRS * bb + u - LAG_NORM, (u - LAG_NORM) % 2
                    dve.wait_ge(ov_full, m + 1)
                    nc.vector.reciprocal(inv_sum[:, v, :], ov[:, SQ:2 * SQ]).then_inc(inv_ready, 1)
                    dve.wait_ge(inv_ready, m + 1)
                    if known(m - 1):
                        dve.wait_ge(y_full, m - 1)
                    tt(OT[:, v, :], ov[:, 0:SQ], inv_sum[:, v, :], ALU.mult).then_inc(ot_ready, 1)
                if has(LAG_APX):
                    v = (u - LAG_APX) % 2
                    for i in range(4):
                        n, bank, free, _ = filled("A", 4 * PAIRS, bb, 4 * (u - LAG_APX) + i)
                        dve.wait_ge(st_full, n + 1)
                        nc.vector.tensor_reduce(neg_max[:, v, i // 2, i % 2:i % 2 + 1], bank[:, 0:SKV], AX.X,
                                                ALU.max, negate=True).then_inc(free, 1)
                if (u - LAG_Y) % PAIRS == PAIRS - 1 and has(LAG_Y):
                    yb_ = (bb + (u - LAG_Y) // PAIRS)
                    dve.wait_ge(y_full, PAIRS * (yb_ + 1))
                    for t in range(QT):
                        row = X[:, bass.ds(QT * yb_ + t, 1), :].rearrange("p a d -> p (a d)")
                        last = nc.vector.scalar_tensor_tensor(row, yb[:, t * D:(t + 1) * D], tanh_g[:, 0:1], row,
                                                              ALU.mult, ALU.add)
                    last.then_inc(y_read, 1)
                if exists(b + 1) and exists(b):
                    if p in L_STEPS:
                        transposed(bb, u // PAIRS + 1, L_STEPS[p], (u // PAIRS + 1) % 2)

            pipeline(dve, step)

        @block.tensor
        def _(pe):
            mm = nc.tensor.matmul

            def split3(out, lhs, rhs):
                for k in range(KD):
                    for i, (a, r) in enumerate(((0, 0), (0, 1), (1, 0))):
                        last = mm(out, lhs(a, k), rhs(r, k), start=(k == 0 and i == 0),
                                  stop=(k == KD - 1 and i == 2))
                return last

            def transposes(bb, j_off, k):
                pe.wait_ge(rows_ready, bb + j_off + 1)
                _, bank, free, value = filled("L", KD, bb, KD * j_off + k)
                pe.wait_ge(free, value)
                for t in range(QT):
                    nc.tensor.transpose(bank[:, t * P:(t + 1) * P], z[:, t, k * P:(k + 1) * P], ident[:])
                nc.tensor.transpose(bank[:, SQ:SKV], z[0:SC, QT, k * P:(k + 1) * P],
                                    ident[0:SC, 0:SC]).then_inc(pj_full, 1)

            def step(bb, u, has):
                b, p, r, w = bb + u // PAIRS, u % PAIRS, u % RING, (u // PAIRS) % 2

                def scores(i):
                    _, bank, free, value = filled("S", NKT * PAIRS, bb, NKT * (u - LAG_S) + i)
                    m = (u - LAG_S) % RING
                    if i == 0:
                        _, _, mfree, mvalue = filled("M", PAIRS, bb, u - LAG_S)
                        pe.wait_ge(mfree, mvalue + 1)
                    pe.wait_ge(free, value)
                    for half in range(2):
                        head, kt = (i, half) if i < 2 else (half, 2)
                        k0, kn = KT[kt]
                        o = bank[0:kn, half * SQ:(half + 1) * SQ]
                        mm(o, KS[:, m, head, 0, k0:k0 + kn], QS[:, m, head, 0, :], start=True, stop=False)
                        last = mm(o, KS[:, m, head, 1, k0:k0 + kn], QS[:, m, head, 1, :], start=False, stop=True)
                    last.then_inc(st_full, 1)

                if has(0):
                    if p == 0:
                        pe.wait_ge(lt_ready, KD * (b + 1))
                    _, bank, free, value = filled("Q", PAIRS, bb, u)
                    pe.wait_ge(free, value)
                    split3(bank[:, 0:SQ], lambda a, k: wq[:, a, k, p * P:(p + 1) * P],
                           lambda a, k: lT[:, w, a, k, 0:SQ]).then_inc(pj_full, 1)
                if has(LAG_S):
                    scores(0)
                if has(0):
                    _, bank, free, value = filled("K", PAIRS, bb, u)
                    pe.wait_ge(free, value)
                    split3(bank[:, 0:SKVE], lambda a, k: wkv[:, a, k, p * P:(p + 1) * P],
                           lambda a, k: lT[:, w, a, k, :]).then_inc(pj_full, 1)
                if has(LAG_S):
                    scores(1)
                if has(LAG_S):
                    scores(2)
                if has(LAG_AV):
                    m, v, q = PAIRS * bb + u - LAG_AV, (u - LAG_AV) % 2, (u - LAG_AV) % PAIRS
                    if known(m):
                        pe.wait_ge(ot_ready, m)
                    part = q // (PAIRS // 2)
                    if q % (PAIRS // 2) == 0:
                        last_v = len(V_STEPS) * ((u - LAG_AV) // PAIRS) + NKT * part + NKT - 1
                        _, _, vfree, vvalue = filled("V", len(V_STEPS), bb, last_v)
                        pe.wait_ge(vfree, vvalue + 1)
                    for kt in range(NKT):
                        kn = KT[kt][1]
                        for half in range(2):
                            slot, col = (half, kt) if kt < 2 else (2, half)
                            _, _, sfree, svalue = filled("S", NKT * PAIRS, bb, NKT * (u - LAG_AV) + slot)
                            pe.wait_ge(sfree, svalue + 1)
                            head = 2 * q + half
                            mm(ov[half * HALF:(half + 1) * HALF, 0:SQ], V[0:kn, kt, head * DH:(head + 1) * DH],
                               probs[0:kn, v, slot, col * SQ:(col + 1) * SQ], start=(kt == 0), stop=(kt == NKT - 1))
                    pe.wait_ge(summed, 2 * m + 2)
                    for half in range(2):
                        last = mm(ov[half * HALF:(half + 1) * HALF, SQ:2 * SQ], ones[:],
                                  prob_sum[:, v, half * SQ:(half + 1) * SQ], start=True, stop=True)
                    last.then_inc(ov_full, 1)
                if p in V_STEPS and has(0):
                    kt, half = V_STEPS[p] % NKT, V_STEPS[p] // NKT
                    k0, kn = KT[kt]
                    _, bank, free, value = filled("V", len(V_STEPS), bb, len(V_STEPS) * (u // PAIRS) + V_STEPS[p])
                    pe.wait_ge(free, value)
                    split3(bank[0:kn, :], lambda a, k: lT[:, w, a, k, k0:k0 + kn],
                           lambda a, k: wkv[:, a, k, INNER + half * 512:INNER + (half + 1) * 512]).then_inc(pj_full, 1)
                if has(LAG_APX):
                    m = (u - LAG_APX) % RING
                    turn = PAIRS // RING
                    pe.wait_ge(q_dup[m], 32 * (turn * bb + (u - LAG_APX) // RING + 1))
                    _, _, kfree, kvalue = filled("K", PAIRS, bb, u - LAG_APX)
                    pe.wait_ge(kfree, kvalue + 1)
                    for i in range(4):
                        head, qt = i // 2, i % 2
                        _, bank, free, value = filled("A", 4 * PAIRS, bb, 4 * (u - LAG_APX) + i)
                        pe.wait_ge(free, value)
                        mm(bank[:, 0:SKVE], QS[:, m, head, 0, qt * P:(qt + 1) * P], KS[:, m, head, 0, :],
                           start=True, stop=True).then_inc(st_full, 1)
                if has(LAG_ROW):
                    _, bank, free, value = filled("M", PAIRS, bb, u - LAG_ROW)
                    pe.wait_ge(free, value)
                    for i in range(4):
                        _, _, afree, avalue = filled("A", 4 * PAIRS, bb, 4 * (u - LAG_ROW) + i)
                        pe.wait_ge(afree, avalue + 1)
                    for qt in range(QT):
                        last = nc.tensor.transpose(bank[0:2, qt * P:(qt + 1) * P],
                                                   neg_max[:, (u - LAG_ROW) % 2, :, qt], ident[:])
                    last.then_inc(pj_full, 1)
                if p in L_STEPS and exists(b + 1) and exists(b):
                    transposes(bb, u // PAIRS + 1, L_STEPS[p])
                if has(LAG_Y):
                    m, v, q = PAIRS * bb + u - LAG_Y, (u - LAG_Y) % 2, (u - LAG_Y) % PAIRS
                    if q == 0 and known(bb + (u - LAG_Y) // PAIRS):
                        pe.wait_ge(y_read, bb + (u - LAG_Y) // PAIRS)
                    pe.wait_ge(ot_ready, m + 1)
                    for t in range(QT):
                        last = mm(yb[:, t * D:(t + 1) * D], OT[:, v, t * P:(t + 1) * P], wo[:, q, :],
                                  start=(q == 0 and t == 0), stop=(q == PAIRS - 1), skip_group_check=True)
                    last.then_inc(y_full, 1)

            pe.wait_ge(tables, 1)
            pe.wait_ge(consts, 6)
            for k in range(KD):
                transposes(0, 0, k)
            pe.wait_ge(w_lo, 3 * KD)
            pe.wait_ge(wo_in, 16)
            pipeline(pe, step)


_INS = ["x", "ctx_1024", "g_xattn", "g_ffn", "L0_xattn_ln1_g", "L0_xattn_ln1_b", "L0_xattn_ln2_g",
        "L0_xattn_ln2_b", "L0_xattn_Wq", "L0_xattn_Wkv", "L0_xattn_Wo", "L0_ffn_router_w",
        "L0_ffn_router_bias", "L0_ffn_expert_gate_w", "L0_ffn_expert_up_w", "L0_ffn_expert_down_w",
        "L0_ffn_conv_w", "L0_ffn_shared_up_w", "L0_ffn_shared_down_w"]


def kernel(**inputs):
    import numpy as np
    import concourse.bacc as bacc
    from concourse.bass_utils import run_bass_kernel_spmd

    nc = bacc.Bacc("TRN2", target_bir_lowering=False, num_devices=1)
    arrays = {f"in_{n}": np.ascontiguousarray(inputs[n]) for n in _INS}
    args = [nc.dram_tensor(n, a.shape, mybir.dt.from_np(a.dtype), kind="ExternalInput").ap()
            for n, a in arrays.items()]
    out = nc.dram_tensor("out", inputs["x"].shape, F32, kind="ExternalOutput").ap()
    build(nc, *args, out)
    return run_bass_kernel_spmd(nc, [arrays], core_ids=[0]).results[0]["out"]
```

```python
from contextlib import ExitStack

import concourse.bass as bass
from concourse import mybir

F32 = mybir.dt.float32
F32R = mybir.dt.float32r
ACT = mybir.ActivationFunctionType
ALU = mybir.AluOpType
AX = mybir.AxisListType

P = 128
HALF = P // 2
NOWHERE = 1e9


def build(nc, x, ctx_in, g_xattn, g_ffn, ln1_g, ln1_b, ln2_g, ln2_b, Wq, Wkv, Wo,
          router_w, router_bias, gate_w, up_w, down_w, conv_w, sh_up, sh_down, out):
    B, SQ, D = x.shape
    SC = ctx_in.shape[1]
    INNER = Wq.shape[1]
    DH = HALF
    H = INNER // DH
    PAIRS = H // 2
    KD = D // P
    QT = SQ // P
    NT = B * QT
    SKV = SQ + SC
    SKVE = SKV + SKV % 2
    KT = [(i * P, min(P, SKV - i * P)) for i in range((SKV + P - 1) // P)]
    NKT = len(KT)
    EPS = 1e-5
    SCALE = 1.0 / float(DH) ** 0.5
    assert NKT == 3 and KD == 2 and QT == 2

    with ExitStack() as keep:
        X = keep.enter_context(nc.sbuf_tensor("X", [P, NT, D], F32))
        ident = keep.enter_context(nc.sbuf_tensor("ident", [P, P], F32))
        tanh_g = keep.enter_context(nc.sbuf_tensor("tanh_g", [P, 2], F32))
        h_stats = keep.enter_context(nc.sbuf_tensor("h_stats", [P, NT, 6], F32))
        E = router_w.shape[1]
        TILES = (2 * B * SQ + E * (P - 1)) // P
        TILES += TILES % 2
        slots_x = nc.dram_tensor("slots_x", (TILES * P, D + 1), F32, kind="Internal").ap()
        routed_y = nc.dram_tensor("routed_y", (2 * B * SQ + TILES * P, D), F32, kind="Internal").ap()
        attention(nc, X, h_stats, ident, tanh_g, x, ctx_in, g_xattn, g_ffn, ln1_g, ln1_b, ln2_g, ln2_b,
                  Wq, Wkv, Wo, slots_x, locals())
        experts(nc, X, h_stats, ident, tanh_g, router_w, router_bias, gate_w, up_w, down_w, conv_w,
                sh_up, sh_down, slots_x, routed_y, out, locals())


def experts(nc, X, h_stats, ident, tanh_g, router_w, router_bias, gate_w, up_w, down_w, conv_w,
            sh_up, sh_down, slots_x, routed_y, out, s):
    B, SQ, D, KD, QT, NT, EPS, E, TILES = (
        s[n] for n in "B SQ D KD QT NT EPS E TILES".split())
    NE = gate_w.shape[0]
    I = gate_w.shape[2]
    KS_ = conv_w.shape[2]
    PAD = KS_ - 1
    U32 = mybir.dt.uint32
    I32 = mybir.dt.int32
    assert I == P and NT * E == 512

    with ExitStack() as c:
        def sb(name, shape, dt=F32):
            return c.enter_context(nc.sbuf_tensor(name, shape, dt))

        def sem(name):
            return c.enter_context(nc.semaphore(name))

        def banks(name, n):
            return [c.enter_context(nc.psum_tensor(f"{name}{i}", [P, 512], F32)) for i in range(n)]

        w_gu = sb("w_gu", [P, NE, KD, 2, I])
        w_dn = sb("w_dn", [P, NE, D])
        conv_raw = sb("conv_raw", [P, D, KS_])
        w_cv = sb("w_cv", [P, KS_, KD, I])
        w_su = sb("w_su", [P, KD, I])
        w_sd = sb("w_sd", [P, D])
        w_rt = sb("w_rt", [P, KD, E])
        bias = sb("bias", [P, E])
        hid = sb("hid", [P, NT, D + 1])
        hT = sb("hT", [P, 2, KD, PAD + SQ])
        h_row = sb("h_row", [P, 2, QT, D])
        h_mv = sb("h_mv", [P, NT, 2])
        h_rstd = sb("h_rstd", [P, NT])
        h_eps = sb("h_eps", [P, NT])
        h_half = sb("h_half", [P, NT])
        act_sh = sb("act_sh", [P, 2, SQ])
        gated = sb("gated", [P, 2, SQ])
        logits = sb("logits", [P, NT, E])
        tri = sb("tri", [P, P])
        all_ones = sb("all_ones", [P, P])
        e_iota = sb("e_iota", [P, E])
        second_half = sb("second_half", [P, NT])
        own_row = sb("own_row", [P, TILES])
        pool_carrier = sb("pool_carrier", [P, 1])
        t_iota = sb("t_iota", [1, TILES])
        ex = sb("ex", [P, NT, E])
        eq = sb("eq", [P, NT, E])
        left = sb("left", [P, NT, E])
        z_sum = sb("z_sum", [P, NT])
        e2 = sb("e2", [P, NT])
        den = sb("den", [P, NT])
        choice = sb("choice", [P, 2, NT])
        best = sb("best", [P, 2, NT])
        w_top = sb("w_top", [P, 2, NT])
        w_id = sb("w_id", [P, 3, NT])
        hot = sb("hot", [P, 3, NT, E])
        scan = sb("scan", [P, 2, NT, E])
        count = sb("count", [P, 4, E])
        count_i = sb("count_i", [P, E], I32)
        slot = sb("slot", [P, NT, E])
        slot_f = sb("slot_f", [P, 2, NT])
        slot_i = sb("slot_i", [P, 2, NT], U32)
        ge = sb("ge", [1, TILES, E])
        tile_f = sb("tile_f", [1, TILES])
        tile_e = sb("tile_e", [1, TILES], I32)
        xs = sb("xs", [P, 4, D + 1])
        goes_to = sb("goes_to", [P, 8], U32)
        xT = sb("xT", [P, 2, D])
        act_e = sb("act_e", [P, 2, I])
        he = sb("he", [P, 2, I])
        heT = sb("heT", [P, 2, I])
        ys = sb("ys", [P, 4, D])
        yg = sb("yg", [P, 4, 2, D])

        pt = banks("pt", 2)
        pg = banks("pg", 2)
        ph = banks("ph", 2)
        py = banks("py", 2)
        tap_bank = [py[0], py[1], ph[0]]

        misc_in = sem("misc_in")
        conv_in = sem("conv_in")
        exp_in = sem("exp_in")
        bconsts = sem("bconsts")
        btables = sem("btables")
        h_var = sem("h_var")
        h_std = sem("h_std")
        hid_ready = sem("hid_ready")
        hid_kept = sem("hid_kept")
        cv_full = sem("cv_full")
        cv_ready = sem("cv_ready")
        t_full = sem("t_full")
        hT_ready = sem("hT_ready")
        rows_back = sem("rows_back")
        t2_full = sem("t2_full")
        hT2_ready = sem("hT2_ready")
        down_full = sem("down_full")
        shared_added = sem("shared_added")
        gu_full = sem("gu_full")
        silu_done = sem("silu_done")
        gated_ready = sem("gated_ready")
        logits_full = sem("logits_full")
        logits_read = sem("logits_read")
        route = sem("route")
        route_exp = sem("route_exp")
        rank_full = sem("rank_full")
        routed = sem("routed")
        tiles_known = sem("tiles_known")
        carried = sem("carried")
        scattered = sem("scattered")
        xs_in = [sem(f"xs_in{i}") for i in range(4)]
        xT_full = sem("xT_full")
        xT_ready = sem("xT_ready")
        goes_ready = sem("goes_ready")
        second_rows = sem("second_rows")
        egu_full = sem("egu_full")
        esilu = sem("esilu")
        he_ready = sem("he_ready")
        heT_full = sem("heT_full")
        heT_ready = sem("heT_ready")
        ey_full = sem("ey_full")
        ey_ready = sem("ey_ready")
        ys_out = [sem(f"ys_out{i}") for i in range(4)]
        yg_in = [sem(f"yg_in{i}") for i in range(4)]
        identity_added = sem("identity_added")
        first_added = sem("first_added")
        route_step = sem("route_step")
        ex_ready = sem("ex_ready")
        final = sem("final")
        stored = sem("stored")

        OFF = 4 * E

        def pipeline(eng, step, tiles, lags, unroll, peeled, tail=0):
            for s_ in range(peeled):
                step(s_, s_ % unroll, [0 <= s_ - n < tiles for n in range(lags)])
            assert (tiles - peeled - tail) % unroll == 0 and peeled % unroll == 0
            with eng.Fori(0, (tiles - peeled - tail) // unroll) as i:
                for u in range(unroll):
                    step(peeled + unroll * i + u, u, [True] * lags)
            for s_ in range(tiles - tail, tiles + lags - 1):
                step(s_, s_ % unroll, [0 <= s_ - n < tiles for n in range(lags)])

        def router_pass(eng, step):
            pipeline(eng, step, B, 3, 2, 4, tail=2)

        def shared_pass(eng, step):
            pipeline(eng, step, B, 3, 2, 4, tail=2)

        def routed_tiles(eng, step):
            pipeline(eng, step, TILES, 4, 8, 8)

        def known(v):
            return not isinstance(v, int) or v >= 1

        def rows_of(t, bt):
            return t[:, bass.ds(bt, 1), :].rearrange("p a d -> p (a d)")

        block = c.enter_context(nc.Block())

        @block.sync
        def _(sp):
            sp.dma_start(conv_raw[:], conv_w).then_inc(conv_in, 16)
            sp.dma_start(w_su[:], sh_up.rearrange("(k p) i -> p k i", p=P)).then_inc(misc_in, 16)
            sp.dma_start(w_sd[:], sh_down).then_inc(misc_in, 16)
            sp.dma_start(w_rt[:], router_w.rearrange("(k p) e -> p k e", p=P)).then_inc(misc_in, 16)
            sp.dma_start(bias[:], router_bias.partition_broadcast(P)).then_inc(misc_in, 16)
            for k in range(KD):
                rows = slice(k * P, (k + 1) * P)
                sp.dma_start(w_gu[:, :, k, 0, :], gate_w[:, rows, :].rearrange("e p i -> p e i")).then_inc(exp_in, 16)
                sp.dma_start(w_gu[:, :, k, 1, :], up_w[:, rows, :].rearrange("e p i -> p e i")).then_inc(exp_in, 16)
            sp.dma_start(w_dn[:], down_w.rearrange("e i d -> i e d")).then_inc(exp_in, 16)
            sp.wait_ge(scattered, 16 * 2 * NT)

            def load(i, u):
                sp.dma_start(xs[:, u], slots_x[bass.ds(i * P, P), :]).then_inc(xs_in[u], 16)

            for i in range(4):
                load(i, i)
            with sp.Fori(0, TILES // 4 - 1) as q:
                for u in range(4):
                    sp.wait_ge(xT_full, 4 * q + u + 1)
                    sp.wait_ge(goes_ready, 4 * q + u + 1)
                    load(4 * q + u + 4, u)
            for u in range(4):
                sp.wait_ge(ys_out[u], 16 * (TILES // 4))
            results = routed_y[0:2 * NT * P, :].rearrange("(i t p) d -> p t i d", i=2, p=P)

            def load_results(t):
                sp.dma_start(yg[:, t % 4], results[:, t]).then_inc(yg_in[t % 4], 16)

            for t in range(4):
                load_results(t)
            for t in range(NT):
                sp.wait_ge(final, t + 1)
                if t + 4 < NT:
                    load_results(t + 4)
                sp.dma_start(out.rearrange("b (q p) d -> p (b q) d", p=P)[:, t, :], X[:, t, :]).then_inc(stored, 16)
            sp.wait_ge(stored, 16 * NT)

        @block.gpsimd
        def _(pool):
            pool.memset(tri[:], 1.0).then_inc(bconsts, 1)
            pool.memset(all_ones[:], 1.0).then_inc(bconsts, 1)
            pool.memset(second_half[:], float(NT * P)).then_inc(bconsts, 1)
            pool.memset(h_eps[:], EPS).then_inc(bconsts, 1)
            pool.memset(h_half[:], -0.5).then_inc(bconsts, 1)
            pool.memset(hT[:].rearrange("p a k t -> p (a k) t")[:, :, 0:PAD], 0.0).then_inc(bconsts, 1)
            pool.iota(e_iota[:], [[1, E]], base=-OFF, channel_multiplier=0,
                      allow_small_or_imprecise_dtypes=True).then_inc(bconsts, 1)
            pool.iota(hid[:, :, D:D + 1], [[P, NT]], base=0, channel_multiplier=1,
                      allow_small_or_imprecise_dtypes=True).then_inc(second_rows, 1)
            pool.iota(own_row[:], [[P, TILES]], base=2 * NT * P, channel_multiplier=1,
                      allow_small_or_imprecise_dtypes=True).then_inc(bconsts, 1)
            pool.iota(t_iota[:], [[P, TILES]], base=0, channel_multiplier=0,
                      allow_small_or_imprecise_dtypes=True).then_inc(bconsts, 1)
            pool.wait_ge(bconsts, 9)
            pool.affine_select(out=tri[:], in_=tri[:], compare_op=ALU.is_gt, fill=0.0, base=0,
                               pattern=[[1, P]], channel_multiplier=-1).then_inc(btables, 1)
            pool.wait_ge(h_var, 1)
            pool.tensor_tensor(h_rstd[:], h_mv[:, :, 1], h_eps[:], ALU.add).then_inc(h_std, 1)
            pool.wait_ge(h_std, 1)
            for tiles in (slice(0, 4 * QT), slice(4 * QT, NT)):
                pool.tensor_tensor(h_rstd[:, tiles], h_rstd[:, tiles], h_half[:, tiles], ALU.pow).then_inc(h_std, 1)
            pool.wait_ge(hid_kept, B)
            pool.wait_ge(routed, 1)
            for i in range(2):
                if i == 1:
                    pool.wait_ge(scattered, 16 * NT)
                    pool.tensor_tensor(hid[:, :, D], hid[:, :, D], second_half[:], ALU.add).then_inc(second_rows, 1)
                pool.wait_ge(second_rows, i + 1)
                for t in range(NT):
                    pool.indirect_dma_start(
                        out=slots_x, out_offset=bass.IndirectOffsetOnAxis(ap=slot_i[:, i, t:t + 1], axis=0),
                        in_=hid[:, t, :], in_offset=None).then_inc(scattered, 16)

            def step(s_, u, live):
                if live[3]:
                    tile8 = (u - 3) % 8
                    pool.wait_ge(ey_ready, s_ - 2)
                    pool.wait_ge(goes_ready, s_ - 2)
                    if known(s_ - 3):
                        pool.wait_ge(carried, s_ - 3)
                    pool.tensor_tensor(pool_carrier[:], h_eps[:, 0:1], h_eps[:, 0:1], ALU.add).then_inc(carried, 1)
                    pool.indirect_dma_start(
                        out=routed_y, out_offset=bass.IndirectOffsetOnAxis(ap=goes_to[:, tile8:tile8 + 1], axis=0),
                        in_=ys[:, tile8 % 4, :], in_offset=None).then_inc(ys_out[tile8 % 4], 16)

            routed_tiles(pool, step)

        @block.scalar
        def _(act):
            def router_step(s_, u, live):
                if live[0]:
                    act.wait_ge(hid_ready, s_ + 1)
                    nc.scalar.activation(hid[:, bass.ds(QT * s_, QT), 0:D], h_row[:, u], ACT.Copy).then_inc(hid_kept, 1)
                    act.wait_ge(t_full, s_ + 1)
                    if known(s_ - 1):
                        act.wait_ge(logits_full, s_ - 1)
                    nc.scalar.activation(hT[:, u, :, PAD:PAD + SQ],
                                         pt[u][:].rearrange("p (k t) -> p k t", k=KD), ACT.Copy).then_inc(hT_ready, 1)

            router_pass(act, router_step)

            def rows_again(b, u):
                nc.scalar.activation(h_row[:, u], hid[:, bass.ds(QT * b, QT), 0:D], ACT.Copy).then_inc(rows_back, 1)

            act.wait_ge(hid_kept, B)
            act.wait_ge(logits_full, B)
            rows_again(0, 0)

            def shared_step(s_, u, live):
                if isinstance(s_, int) and s_ == 2:
                    act.wait_ge(ex_ready, 1)
                    nc.scalar.activation(ex[:], ex[:], ACT.Exp).then_inc(route_exp, 1)
                    nc.scalar.activation(e2[:], e2[:], ACT.Exp).then_inc(route_exp, 1)
                if live[0]:
                    act.wait_ge(t2_full, s_ + 1)
                    if known(s_ - 1):
                        act.wait_ge(gu_full, s_ - 1)
                    nc.scalar.activation(hT[:, u, :, PAD:PAD + SQ],
                                         pt[u][:].rearrange("p (k t) -> p k t", k=KD), ACT.Copy).then_inc(hT2_ready, 1)
                    if not isinstance(s_, int) or s_ + 1 < B:
                        rows_again(s_ + 1, (u + 1) % 2)
                if live[1]:
                    v = (u - 1) % 2
                    act.wait_ge(gu_full, s_)
                    if known(s_ - 2):
                        act.wait_ge(gated_ready, s_ - 2)
                    nc.scalar.activation(act_sh[:, v, :], pg[v][:, 0:SQ], ACT.Silu).then_inc(silu_done, 1)

            shared_pass(act, shared_step)

            def step(s_, u, live):
                if live[1]:
                    v = (u - 1) % 2
                    act.wait_ge(egu_full, s_)
                    if known(s_ - 2):
                        act.wait_ge(he_ready, s_ - 2)
                    nc.scalar.activation(act_e[:, v, :], pg[v][:, 0:I], ACT.Silu).then_inc(esilu, 1)
                if live[2]:
                    v = u % 2
                    act.wait_ge(heT_full, s_ - 1)
                    if known(s_ - 3):
                        act.wait_ge(ey_full, s_ - 3)
                    nc.scalar.activation(heT[:, v, :], ph[v][:, 0:I], ACT.Copy).then_inc(heT_ready, 1)

            routed_tiles(act, step)

        @block.vector
        def _(dve):
            tt, ts = nc.vector.tensor_tensor, nc.vector.tensor_scalar

            for t in range(NT):
                last = nc.vector.bn_aggr(h_mv[:, t, :], h_stats[:, t, :])
            last.then_inc(h_var, 1)
            dve.wait_ge(bconsts, 9)
            for j in range(KS_):
                dve.wait_ge(cv_full, j + 1)
                nc.vector.tensor_copy(w_cv[:, j, :, :],
                                      tap_bank[j][:, 0:KD * I].rearrange("p (k i) -> p k i", k=KD)
                                      ).then_inc(cv_ready, 1)
            dve.wait_ge(misc_in, 16 * 4)

            def router_step(s_, u, live):
                if live[0]:
                    if known(s_ - 1):
                        dve.wait_ge(hid_kept, s_ - 1)
                        dve.wait_ge(t_full, s_ - 1)
                    if isinstance(s_, int) and s_ == 4 or not isinstance(s_, int):
                        dve.wait_ge(h_std, 3)
                    for t in range(QT):
                        n = QT * s_ + t
                        last = ts(h_row[:, u, t, :], rows_of(X, n), rows_of(h_mv, n)[:, 0:1],
                                  h_rstd[:, bass.ds(n, 1)], ALU.subtract, ALU.mult)
                    last.then_inc(hid_ready, 1)
                if live[2]:
                    dve.wait_ge(logits_full, s_ - 1)
                    tt(logits[:, bass.ds(QT * (s_ - 2), QT), :],
                       ph[u][:, 0:QT * E].rearrange("p (t e) -> p t e", t=QT),
                       bias[:].unsqueeze(1).to_broadcast([P, QT, E]), ALU.add).then_inc(logits_read, 1)

            dve.wait_ge(h_std, 2)
            router_pass(dve, router_step)

            steps = [0]

            def then(ins):
                steps[0] += 1
                ins.then_inc(route_step, 1)
                dve.wait_ge(route_step, steps[0])

            def over_e(v):
                return v.unsqueeze(2).to_broadcast([P, NT, E])

            def over_t(v):
                return v.unsqueeze(1).to_broadcast([P, NT, E])

            dve.wait_ge(logits_read, B)
            dve.wait_ge(hid_kept, B)
            for i in range(2):
                src = logits if i == 0 else left
                then(nc.vector.tensor_reduce(best[:, i, :], src[:], AX.X, ALU.max))
                then(tt(eq[:], src[:], over_e(best[:, i, :]), ALU.is_equal))
                then(tt(eq[:], eq[:], over_t(e_iota[:]), ALU.mult))
                then(nc.vector.tensor_reduce(choice[:, i, :], eq[:], AX.X, ALU.min))
                then(tt(hot[:, i], over_t(e_iota[:]), over_e(choice[:, i, :]), ALU.is_equal))
                if i == 0:
                    then(nc.vector.scalar_tensor_tensor(left[:], hot[:, 0], -1e38, logits[:], ALU.mult, ALU.add))
            tt(hot[:, 2], hot[:, 0], hot[:, 1], ALU.add).then_inc(route, 1)
            in_tile = py[0][:].rearrange("p (t e) -> p t e", e=E)
            of_tile = py[1][:].rearrange("p (t e) -> p t e", e=E)
            dve.wait_ge(rank_full, 1)
            then(nc.vector.tensor_copy(scan[:, 0], of_tile))
            cur, d = 0, 1
            while d < NT:
                nc.vector.tensor_copy(scan[:, 1 - cur, 0:d, :], scan[:, cur, 0:d, :])
                then(tt(scan[:, 1 - cur, d:NT, :], scan[:, cur, d:NT, :], scan[:, cur, 0:NT - d, :], ALU.add))
                cur, d = 1 - cur, 2 * d
            total = scan[:, cur, NT - 1, :]
            shift = P.bit_length() - 1
            then(ts(count_i[:], total, float(P - 1), None, ALU.add))
            then(ts(count_i[:], count_i[:], shift, shift, ALU.logical_shift_right, ALU.logical_shift_left))
            nc.vector.tensor_copy(count[:, 0, :], count_i[:])
            then(nc.vector.tensor_copy(count[:, 1, :], count_i[:]))
            a, b_, d = 1, 2, 1
            while d < E:
                nc.vector.tensor_copy(count[:, b_, 0:d], count[:, a, 0:d])
                then(tt(count[:, b_, d:E], count[:, a, d:E], count[:, a, 0:E - d], ALU.add))
                a, b_, d = b_, a, 2 * d
            ends = count[:, a, :]
            then(tt(count[:, 3, :], ends, count[:, 0, :], ALU.subtract))
            then(tt(slot[:], in_tile, scan[:, cur], ALU.add))
            then(tt(slot[:], slot[:], over_t(count[:, 3, :]), ALU.add))
            then(tt(slot[:], of_tile, slot[:], ALU.subtract))
            for i in range(2):
                then(tt(eq[:], hot[:, i], slot[:], ALU.mult))
                then(nc.vector.tensor_reduce(slot_f[:, i, :], eq[:], AX.X, ALU.add))
            ts(slot_i[:], slot_f[:], -1.0, None, ALU.mult).then_inc(routed, 1)

            tt(e2[:], best[:, 1, :], best[:, 0, :], ALU.subtract)
            tt(ex[:], logits[:], over_e(best[:, 0, :]), ALU.subtract).then_inc(ex_ready, 1)
            dve.wait_ge(route_exp, 2)
            then(nc.vector.tensor_reduce(z_sum[:], ex[:], AX.X, ALU.add))
            then(nc.vector.scalar_tensor_tensor(den[:], z_sum[:], 1e-6, e2[:], ALU.mult, ALU.add))
            then(ts(den[:], den[:], 1.0, None, ALU.add))
            then(nc.vector.reciprocal(w_top[:, 0, :], den[:]))
            then(ts(w_top[:, 0, :], w_top[:, 0, :], tanh_g[:, 1:2], None, ALU.mult))
            then(tt(w_top[:, 1, :], w_top[:, 0, :], e2[:], ALU.mult))
            then(ts(w_id[:, 0:2, :], choice[:], float(E - 1 - OFF), None, ALU.is_equal))
            then(tt(w_id[:, 0:2, :], w_id[:, 0:2, :], w_top[:], ALU.mult))
            tt(w_top[:], w_top[:], w_id[:, 0:2, :], ALU.subtract)
            then(tt(w_id[:, 2, :], w_id[:, 0, :], w_id[:, 1, :], ALU.add))

            then(tt(ge[:], count[0:1, a, :].unsqueeze(1).to_broadcast([1, TILES, E]),
                    t_iota[:].unsqueeze(2).to_broadcast([1, TILES, E]), ALU.is_le))
            then(nc.vector.tensor_reduce(tile_f[:], ge[:], AX.X, ALU.add))
            ts(tile_e[:], tile_f[:], float(NE - 1), None, ALU.min).then_inc(tiles_known, 1)
            def shared_step(s_, u, live):
                if live[1]:
                    v = (u - 1) % 2
                    dve.wait_ge(silu_done, s_)
                    if known(s_ - 2):
                        dve.wait_ge(down_full, s_ - 2)
                    tt(gated[:, v, :], pg[v][:, SQ:2 * SQ], act_sh[:, v, :], ALU.mult).then_inc(gated_ready, 1)
                    for t in range(QT):
                        n = QT * (s_ - 1) + t
                        last = nc.vector.scalar_tensor_tensor(rows_of(X, n), rows_of(hid, n)[:, 0:D],
                                                              w_id[:, 2, bass.ds(n, 1)], rows_of(X, n),
                                                              ALU.mult, ALU.add)
                    last.then_inc(identity_added, 1)
                if live[2]:
                    dve.wait_ge(down_full, s_ - 1)
                    dve.wait_ge(identity_added, s_ - 1)
                    for t in range(QT):
                        row = rows_of(X, QT * (s_ - 2) + t)
                        last = nc.vector.scalar_tensor_tensor(row, py[u][:, t * D:(t + 1) * D], tanh_g[:, 1:2], row,
                                                              ALU.mult, ALU.add)
                    last.then_inc(shared_added, 1)

            shared_pass(dve, shared_step)

            def step(s_, u, live):
                if live[0]:
                    v = u % 2
                    dve.wait_ge(xT_full, s_ + 1)
                    if known(s_ - 1):
                        dve.wait_ge(egu_full, s_ - 1)
                    nc.vector.tensor_copy(xT[:, v, :], pt[v][:, 0:D]).then_inc(xT_ready, 1)
                    tt(goes_to[:, u:u + 1], xs[:, u % 4, D:D + 1], own_row[:, bass.ds(s_, 1)], ALU.min
                       ).then_inc(goes_ready, 1)
                if live[1]:
                    v = (u - 1) % 2
                    dve.wait_ge(esilu, s_)
                    if known(s_ - 2):
                        dve.wait_ge(heT_full, s_ - 2)
                    tt(he[:, v, :], pg[v][:, I:2 * I], act_e[:, v, :], ALU.mult).then_inc(he_ready, 1)
                if live[3]:
                    v, r = (u - 3) % 2, (u - 3) % 4
                    dve.wait_ge(ey_full, s_ - 2)
                    turns = 16 * ((s_ - 3) // 4) if isinstance(s_, int) else 4 * (s_ - 3 - r)
                    if known(turns):
                        dve.wait_ge(ys_out[r], turns)
                    nc.vector.tensor_copy(ys[:, r, :], py[v][:, 0:D]).then_inc(ey_ready, 1)

            routed_tiles(dve, step)

            def add(t, i):
                return nc.vector.scalar_tensor_tensor(X[:, t, :], yg[:, t % 4, i, :], w_top[:, i, t:t + 1],
                                                      X[:, t, :], ALU.mult, ALU.add)

            for t in range(NT + 1):
                if t < NT:
                    dve.wait_ge(yg_in[t % 4], 16 * (t // 4 + 1))
                    add(t, 0).then_inc(first_added, 1)
                if t:
                    dve.wait_ge(first_added, t)
                    add(t - 1, 1).then_inc(final, 1)

        @block.tensor
        def _(pe):
            pe.wait_ge(conv_in, 16)
            for j in range(KS_):
                for k in range(KD):
                    last = nc.tensor.transpose(tap_bank[j][:, k * I:(k + 1) * I],
                                               conv_raw[:, k * P:(k + 1) * P, j], ident[:])
                last.then_inc(cv_full, 1)
            pe.wait_ge(misc_in, 16 * 4)
            pe.wait_ge(bconsts, 9)
            pe.wait_ge(btables, 1)
            pe.wait_ge(cv_ready, KS_)

            def transposes(u, full):
                for t in range(QT):
                    for k in range(KD):
                        last = nc.tensor.transpose(pt[u][:, k * SQ + t * P:k * SQ + (t + 1) * P],
                                                   h_row[:, u, t, k * P:(k + 1) * P], ident[:])
                last.then_inc(full, 1)

            def router_step(s_, u, live):
                if live[0]:
                    pe.wait_ge(hid_ready, s_ + 1)
                    if known(s_ - 1):
                        pe.wait_ge(hT_ready, s_ - 1)
                    transposes(u, t_full)
                if live[1]:
                    v = (u - 1) % 2
                    pe.wait_ge(hT_ready, s_)
                    if known(s_ - 2):
                        pe.wait_ge(logits_read, s_ - 2)
                    for t in range(QT):
                        for k in range(KD):
                            last = nc.tensor.matmul(ph[v][:, t * E:(t + 1) * E],
                                                    hT[:, v, k, PAD + t * P:PAD + (t + 1) * P], w_rt[:, k, :],
                                                    start=(k == 0), stop=(k == KD - 1))
                    last.then_inc(logits_full, 1)

            router_pass(pe, router_step)

            def shared_step(s_, u, live):
                if live[0]:
                    pe.wait_ge(rows_back, s_ + 1)
                    if known(s_ - 1):
                        pe.wait_ge(hT2_ready, s_ - 1)
                    transposes(u, t2_full)
                if live[1]:
                    v = (u - 1) % 2
                    pe.wait_ge(hT2_ready, s_)
                    if known(s_ - 2):
                        pe.wait_ge(gated_ready, s_ - 2)
                    taps = [(k, j) for k in range(KD) for j in range(KS_)]
                    for n, (k, j) in enumerate(taps):
                        nc.tensor.matmul(pg[v][:, 0:SQ], w_cv[:, j, k, :], hT[:, v, k, j:j + SQ],
                                         start=(n == 0), stop=(n == len(taps) - 1))
                    for k in range(KD):
                        last = nc.tensor.matmul(pg[v][:, SQ:2 * SQ], w_su[:, k, :], hT[:, v, k, PAD:PAD + SQ],
                                                start=(k == 0), stop=(k == KD - 1))
                    last.then_inc(gu_full, 1)
                if isinstance(s_, int) and s_ == 1:
                    pe.wait_ge(route, 1)
                    flat = hot[:, 2].rearrange("p t e -> p (t e)")
                    nc.tensor.matmul(py[0][:], tri[:], flat, start=True, stop=True)
                    nc.tensor.matmul(py[1][:], all_ones[:], flat, start=True, stop=True).then_inc(rank_full, 1)
                if live[2]:
                    pe.wait_ge(gated_ready, s_ - 1)
                    if known(s_ - 3):
                        pe.wait_ge(shared_added, s_ - 3)
                    for t in range(QT):
                        last = nc.tensor.matmul(py[u][:, t * D:(t + 1) * D], gated[:, u, t * P:(t + 1) * P], w_sd[:],
                                                start=True, stop=True)
                    last.then_inc(down_full, 1)

            shared_pass(pe, shared_step)
            pe.wait_ge(tiles_known, 1)
            pe.wait_ge(shared_added, B)
            pe.wait_ge(exp_in, 16 * (2 * KD + 1))

            expert_reg = [pe.alloc_register(f"expert{i}") for i in range(4)]

            def fetch_expert(tile, r):
                pe.reg_load(expert_reg[r], tile_e[0:1, bass.ds(tile, 1)])

            def expert_of(r):
                return pe.snap(expert_reg[r], min_val=0, max_val=NE - 1)

            fetch_expert(0, 0)

            def step(s_, u, live):
                if live[0]:
                    v = u % 2
                    pe.wait_ge(xs_in[u % 4], 16 * (s_ // 4 + 1) if isinstance(s_, int) else 4 * (s_ - u % 4 + 4))
                    if known(s_ - 1):
                        pe.wait_ge(xT_ready, s_ - 1)
                    for k in range(KD):
                        last = nc.tensor.transpose(pt[v][:, k * P:(k + 1) * P], xs[:, u % 4, k * P:(k + 1) * P], ident[:])
                    last.then_inc(xT_full, 1)
                if live[1]:
                    v = (u - 1) % 2
                    e = expert_of((u - 1) % 4)
                    pe.wait_ge(xT_ready, s_)
                    if known(s_ - 2):
                        pe.wait_ge(he_ready, s_ - 2)
                    for k in range(KD):
                        last = nc.tensor.matmul(pg[v][:, 0:2 * I], xT[:, v, k * P:(k + 1) * P],
                                                w_gu[:, bass.ds(e, 1), k].rearrange("p a g i -> p (a g i)"),
                                                start=(k == 0), stop=(k == KD - 1))
                    last.then_inc(egu_full, 1)
                if live[0] and known(s_):
                    fetch_expert(s_, u % 4)
                if live[2]:
                    v = u % 2
                    pe.wait_ge(he_ready, s_ - 1)
                    if known(s_ - 3):
                        pe.wait_ge(heT_ready, s_ - 3)
                    nc.tensor.transpose(ph[v][:, 0:I], he[:, v, :], ident[:]).then_inc(heT_full, 1)
                if live[3]:
                    v = (u - 3) % 2
                    e = expert_of((u - 3) % 4)
                    pe.wait_ge(heT_ready, s_ - 2)
                    if known(s_ - 4):
                        pe.wait_ge(ey_ready, s_ - 4)
                    nc.tensor.matmul(py[v][:, 0:D], heT[:, v, :],
                                     w_dn[:, bass.ds(e, 1), :].rearrange("p a d -> p (a d)"),
                                     start=True, stop=True).then_inc(ey_full, 1)

            routed_tiles(pe, step)


def attention(nc, X, h_stats, ident, tanh_g, x, ctx_in, g_xattn, g_ffn, ln1_g, ln1_b, ln2_g, ln2_b,
              Wq, Wkv, Wo, slots_x, s):
    B, SQ, D, SC, INNER, DH, H, PAIRS, KD, QT, SKV, SKVE, KT, NKT, EPS, SCALE = (
        s[n] for n in "B SQ D SC INNER DH H PAIRS KD QT SKV SKVE KT NKT EPS SCALE".split())
    N = B * PAIRS
    UNROLL = 2 * PAIRS
    LAG_APX, LAG_ROW, LAG_S, LAG_AV, LAG_NORM, LAG_Y = 1, 2, 3, 4, 4, 5
    RING = 4
    V_STEPS = {0: 0, 1: 1, 2: 2, 4: 3, 5: 4, 6: 5}
    CLEARED = slots_x.shape[0] // P // B
    assert CLEARED * B * P == slots_x.shape[0] and CLEARED <= PAIRS
    L_STEPS = {3: 0, 4: 1}

    with ExitStack() as c:
        def sb(name, shape, dt=F32):
            return c.enter_context(nc.sbuf_tensor(name, shape, dt))

        def sem(name):
            return c.enter_context(nc.semaphore(name))

        def banks(name, n):
            return [c.enter_context(nc.psum_tensor(f"{name}{i}", [P, 512], F32)) for i in range(n)]

        wq = sb("wq", [P, 2, KD, INNER], F32R)
        wkv = sb("wkv", [P, 2, KD, 2 * INNER], F32R)
        wo = sb("wo", [P, PAIRS, D])
        stage = sb("stage", [P, 2, INNER])
        gb = sb("gb", [P, 4, KD])
        ones = sb("ones", [P, DH])
        neg_half = sb("neg_half", [P, 4])
        eps = sb("eps", [P, 4])
        carrier = sb("carrier", [P, 1])
        zeros = sb("zeros", [P, D + 1])
        ctx_t = sb("ctx_t", [P, D])
        z = sb("z", [P, QT + 1, D])
        stats = sb("stats", [P, QT + 1, 6])
        mv = sb("mv", [P, 2, QT + 1, 2])
        rstd = sb("rstd", [P, 2, QT + 1])
        lT32 = sb("lT32", [P, KD, SKVE])
        lT = sb("lT", [P, 2, 2, KD, SKVE], F32R)
        KS = sb("KS", [P, RING, 2, 2, SKVE], F32R)
        QS = sb("QS", [P, RING, 2, 2, SQ], F32R)
        V = sb("V", [P, NKT, INNER])
        neg_max = sb("neg_max", [P, 2, 2, QT])
        probs = sb("probs", [P, 2, NKT, 2 * SQ])
        prob_sum = sb("prob_sum", [P, 2, 2 * SQ])
        inv_sum = sb("inv_sum", [P, 2, SQ])
        OT = sb("OT", [P, 2, SQ])

        pj = banks("pj", 2)
        st = banks("st", 4)
        ov = banks("ov", 1)[0]
        yb = banks("yb", 1)[0]

        x_in = sem("x_in")
        x_rest = sem("x_rest")
        ctx_loaded = sem("ctx_loaded")
        ctx_used = sem("ctx_used")
        ln_in = sem("ln_in")
        gate_in = sem("gate_in")
        w_in = [sem("w_in0"), sem("w_in1")]
        wo_in = sem("wo_in")
        w_hi = sem("w_hi")
        w_lo = sem("w_lo")
        consts = sem("consts")
        tables = sem("tables")
        one_rows = sem("one_rows")
        gates = sem("gates")
        zeros_set = sem("zeros_set")
        slots_clear = sem("slots_clear")
        ln_dve = sem("ln_dve")
        ln_rstd = sem("ln_rstd")
        ln_chain = sem("ln_chain")
        rows_ready = sem("rows_ready")
        lt_ready = sem("lt_ready")
        pj_full = sem("pj_full")
        pj_free = [sem(f"pj_free{i}") for i in range(len(pj))]
        q_hi = sem("q_hi")
        k_hi = sem("k_hi")
        q_dup = [sem(f"q_dup{i}") for i in range(RING)]
        st_full = sem("st_full")
        st_free = [sem(f"st_free{i}") for i in range(len(st))]
        summed = sem("summed")
        ov_full = sem("ov_full")
        inv_ready = sem("inv_ready")
        ot_ready = sem("ot_ready")
        y_full = sem("y_full")
        y_read = sem("y_read")

        def fills(n):
            b, p = divmod(n, PAIRS)
            order = []

            def lagged(lag, ring, kind, per, i):
                if 0 <= n - lag < N:
                    order.append((ring, kind, per * (n - lag) + i))

            lagged(0, 0, "Q", 1, 0)
            lagged(LAG_S, 1, "S", NKT, 0)
            lagged(0, 0, "K", 1, 0)
            lagged(LAG_S, 1, "S", NKT, 1)
            lagged(LAG_S, 1, "S", NKT, 2)
            for i in range(4):
                lagged(LAG_APX, 1, "A", 4, i)
            if p in V_STEPS and b < B:
                order.append((0, "V", len(V_STEPS) * b + V_STEPS[p]))
            lagged(LAG_ROW, 0, "M", 1, 0)
            if p in L_STEPS and b + 1 < B:
                order.append((0, "L", KD * (b + 1) + L_STEPS[p]))
            return order

        number, rings = {}, (pj, st)
        totals = [KD, 0]
        for k in range(KD):
            number["L", k] = k
        in_loop = [0, 0]
        for n in range(N + LAG_Y + 2):
            for ring, kind, i in fills(n):
                number[kind, i] = totals[ring]
                totals[ring] += 1
                in_loop[ring] += UNROLL <= n < 2 * UNROLL
        frees = (pj_free, st_free)
        assert all(f % (2 * len(r)) == 0 for f, r in zip(in_loop, rings))

        def filled(kind, per, bb, off):
            ring = 0 if kind in "QKVML" else 1
            size, a_batch = len(rings[ring]), in_loop[ring] // 2
            if isinstance(bb, int):
                n = number[kind, per * bb + off]
                return n, rings[ring][n % size], frees[ring][n % size], n // size + 1
            n = number[kind, 2 * per + off]
            assert number[kind, 4 * per + off] == n + 2 * a_batch
            return (a_batch * (bb - 2) + n, rings[ring][n % size], frees[ring][n % size],
                    a_batch // size * (bb - 2) + (n // size + 1))

        def pipeline(eng, step):
            def written_out(n):
                bb = n // UNROLL * 2
                step(bb, n - PAIRS * bb, lambda lag: 0 <= n - lag < N)

            for n in range(UNROLL):
                written_out(n)
            with eng.Fori(0, (N - 2 * UNROLL) // UNROLL) as i:
                for u in range(UNROLL):
                    step(2 * i + 2, u, lambda lag: True)
            for n in range(N - UNROLL, N + LAG_Y + 2):
                written_out(n)

        def exists(b):
            return not isinstance(b, int) or b < B

        def known(v):
            return not isinstance(v, int) or v >= 1

        block = c.enter_context(nc.Block())

        @block.sync
        def _(sp):
            sp.dma_start(ctx_t[0:SC, :], ctx_in[0]).then_inc(ctx_loaded, 16)
            rows = x.rearrange("b (q p) d -> p (b q) d", p=P)
            first = slice(0, 2 * QT)
            sp.dma_start(X[:, first, :], rows[:, first, :]).then_inc(x_in, 16)
            for i, v in enumerate((ln1_g, ln1_b, ln2_g, ln2_b)):
                sp.dma_start(gb[:, i, :], v.rearrange("(k p) -> p k", p=P),
                             allow_slow_non_contiguous=True).then_inc(ln_in, 16)
            pieces = [(Wq, k, 0) for k in range(KD)] + [(Wkv, k, n) for n in range(2) for k in range(KD)]
            for i, (w, k, n) in enumerate(pieces):
                if i >= 2:
                    sp.wait_ge(w_lo, i - 1)
                sp.dma_start(stage[:, i % 2, :], w[k * P:(k + 1) * P, n * INNER:(n + 1) * INNER]
                             ).then_inc(w_in[i % 2], 16)
            sp.dma_start(wo[:], Wo.rearrange("(q p) d -> p q d", p=P)).then_inc(wo_in, 16)
            for q in range(1, 4):
                part = slice(q * B // 4 * QT if q > 1 else 2 * QT, (q + 1) * B // 4 * QT)
                sp.dma_start(X[:, part, :], rows[:, part, :]).then_inc(x_rest, 16)
            sp.wait_ge(zeros_set, 2)

            def step(bb, u, has):
                r = u % RING
                if has(0):
                    sp.wait_ge(q_hi, PAIRS * bb + u + 1)
                    sp.dma_start(QS[HALF:P, r, 0, 0].bitcast(F32), QS[0:HALF, r, 0, 0].bitcast(F32)
                                 ).then_inc(q_dup[r], 16)
                    sp.dma_start(QS[0:HALF, r, 1, 0].bitcast(F32), QS[HALF:P, r, 1, 0].bitcast(F32)
                                 ).then_inc(q_dup[r], 16)
                b = bb + u // PAIRS
                if u % PAIRS < CLEARED and exists(b):
                    sp.dma_start(slots_x[bass.ds((CLEARED * b + u % PAIRS) * P, P), :], zeros[:]
                                 ).then_inc(slots_clear, 16)
                if u % PAIRS == 6 and exists(b + 2):
                    sp.wait_ge(ctx_used, b + 2)
                    sp.dma_start(ctx_t[0:SC, :], ctx_in[bass.ds(b + 2, 1)].rearrange("a s d -> (a s) d")
                                 ).then_inc(ctx_loaded, 16)

            sp.wait_ge(ctx_used, 1)
            sp.dma_start(ctx_t[0:SC, :], ctx_in[1]).then_inc(ctx_loaded, 16)
            pipeline(sp, step)
            sp.wait_ge(slots_clear, 16 * CLEARED * B)

        @block.gpsimd
        def _(pool):
            pool.memset(ident[:], 0.0).then_inc(consts, 1)
            pool.memset(ones[:], 1.0).then_inc(consts, 1)
            pool.memset(neg_half[:], -0.5).then_inc(consts, 1)
            pool.memset(eps[:], EPS).then_inc(consts, 1)
            pool.memset(mv[:].rearrange("p a t s -> p (a t s)"), 1.0).then_inc(consts, 1)
            pool.memset(lT32[:, :, SKV:SKVE], 0.0).then_inc(consts, 1)
            pool.wait_ge(consts, 1)
            pool.affine_select(out=ident[:], in_=ident[:], compare_op=ALU.not_equal, fill=1.0, base=0,
                               pattern=[[-1, P]], channel_multiplier=1).then_inc(tables, 1)
            pool.memset(zeros[:, 0:D], 0.0).then_inc(zeros_set, 1)
            pool.memset(zeros[:, D:D + 1], NOWHERE).then_inc(zeros_set, 1)
            pool.wait_ge(consts, 6)

            def inv_std(j, which, n):
                pool.wait_ge(ln_dve, 2 * j + 1 + which)
                pool.tensor_tensor(rstd[:, which, 0:n], mv[:, which, 0:n, 1], eps[:, 0:n], ALU.add
                                   ).then_inc(ln_rstd, 1)
                pool.wait_ge(ln_rstd, 4 * j + 2 * which + 1)
                pool.tensor_tensor(rstd[:, which, 0:n], rstd[:, which, 0:n], neg_half[:, 0:n], ALU.pow
                                   ).then_inc(ln_rstd, 1)

            def step(bb, u, has):
                b, p = bb + u // PAIRS, u % PAIRS
                if has(LAG_AV):
                    m, v = PAIRS * bb + u - LAG_AV, (u - LAG_AV) % 2
                    for i in range(NKT):
                        _, _, free, value = filled("S", NKT * PAIRS, bb, NKT * (u - LAG_AV) + i)
                        pool.wait_ge(free, value + 1)
                    if known(m - 1):
                        pool.wait_ge(ov_full, m - 1)
                    total = prob_sum[:, v, :].rearrange("p (h q) -> p h q", h=2)
                    pool.tensor_tensor(total, probs[:, v, 0:2, 0:SQ], probs[:, v, 0:2, SQ:2 * SQ], ALU.add
                                       ).then_inc(summed, 1)
                    pool.wait_ge(summed, 2 * m + 1)
                    kn = KT[2][1]
                    pool.tensor_tensor(prob_sum[0:kn, v, :], prob_sum[0:kn, v, :], probs[0:kn, v, 2, :], ALU.add
                                       ).then_inc(summed, 1)
                if p < 2 and exists(b + 1) and exists(b):
                    inv_std(b + 1, p, QT + 1 - p)

            inv_std(0, 0, QT + 1)
            inv_std(0, 1, QT)
            pipeline(pool, step)

        @block.scalar
        def _(act):
            act.dma_start(tanh_g[:, 0:1], g_xattn.partition_broadcast(P)).then_inc(gate_in, 16)
            act.dma_start(tanh_g[:, 1:2], g_ffn.partition_broadcast(P)).then_inc(gate_in, 16)
            hi = [wq[:, 0, k, :] for k in range(KD)] + \
                 [wkv[:, 0, k, n * INNER:(n + 1) * INNER] for n in range(2) for k in range(KD)]
            for i, w in enumerate(hi):
                act.wait_ge(w_in[i % 2], 16 * (i // 2 + 1))
                nc.scalar.activation(w, stage[:, i % 2, :], ACT.Copy).then_inc(w_hi, 1)
            act.wait_ge(gate_in, 32)
            nc.scalar.activation(tanh_g[:], tanh_g[:], ACT.Tanh).then_inc(gates, 1)
            act.wait_ge(one_rows, 1)

            def step(bb, u, has):
                b, p, r = bb + u // PAIRS, u % PAIRS, u % RING
                copy = nc.scalar.activation

                def exp(i):
                    v = (u - LAG_S) % 2
                    n, bank, free, _ = filled("S", NKT * PAIRS, bb, NKT * (u - LAG_S) + i)
                    m = PAIRS * bb + u - LAG_S
                    if i == 0 and known(m - 1):
                        act.wait_ge(ov_full, m - 1)
                    kn = KT[2][1] if i == 2 else P
                    act.wait_ge(st_full, n + 1)
                    nc.scalar.activation(probs[0:kn, v, i, :], bank[0:kn, :], ACT.Exp, scale=SCALE).then_inc(free, 1)

                if has(0):
                    n, bank, _, _ = filled("Q", PAIRS, bb, u)
                    act.wait_ge(pj_full, n + 1)
                    copy(QS[0:HALF, r, 0, 0, :], bank[0:HALF, 0:SQ], ACT.Copy)
                    copy(QS[HALF:P, r, 1, 0, :], bank[HALF:P, 0:SQ], ACT.Copy).then_inc(q_hi, 1)
                if has(LAG_S):
                    exp(0)
                if has(0):
                    n, bank, _, _ = filled("K", PAIRS, bb, u)
                    act.wait_ge(pj_full, n + 1)
                    for half in range(2):
                        rows = slice(half * HALF, (half + 1) * HALF)
                        last = copy(KS[rows, r, half, :, :],
                                    bank[rows, 0:SKVE].unsqueeze(1).to_broadcast([HALF, 2, SKVE]), ACT.Copy)
                    last.then_inc(k_hi, 1)
                if has(LAG_S):
                    exp(1)
                    exp(2)
                if p in V_STEPS and has(0):
                    kt, half = V_STEPS[p] % NKT, V_STEPS[p] // NKT
                    kn = KT[kt][1]
                    n, bank, free, _ = filled("V", len(V_STEPS), bb, len(V_STEPS) * (u // PAIRS) + V_STEPS[p])
                    act.wait_ge(pj_full, n + 1)
                    copy(V[0:kn, kt, half * 512:(half + 1) * 512], bank[0:kn, :], ACT.Copy).then_inc(free, 1)
                if has(LAG_ROW):
                    n, bank, free, _ = filled("M", PAIRS, bb, u - LAG_ROW)
                    r = (u - LAG_ROW) % RING
                    act.wait_ge(pj_full, n + 1)
                    copy(QS[HALF:HALF + 2, r, 0, 1, :], bank[0:2, 0:SQ], ACT.Copy)
                    copy(QS[0:2, r, 1, 1, :], bank[0:2, 0:SQ], ACT.Copy).then_inc(free, 1)

            pipeline(act, step)

        @block.vector
        def _(dve):
            tt = nc.vector.tensor_tensor
            for bank in pj_free + st_free:
                dve.sem_inc(bank, 1)
            nc.vector.memset(QS[:, :, :, 1, :].bitcast(F32), 0.0)
            nc.vector.memset(KS[:, :, :, 1, :].bitcast(F32), 0.0)
            dve.wait_ge(tables, 1)

            def layer_norm(j, part, v):
                src = [X[:, bass.ds(QT * j + t, 1), :].rearrange("p a d -> p (a d)") for t in range(QT)]
                C = 2 + KD
                if part == 0:
                    dve.wait_ge(ctx_loaded, 16 * (j + 1))
                    if isinstance(j, int) and j == 2:
                        dve.wait_ge(x_rest, 16 * 3)
                    for t in range(QT):
                        nc.vector.bn_stats(stats[:, t, :], src[t])
                    nc.vector.bn_stats(stats[0:SC, QT, :], ctx_t[0:SC, :]).then_inc(ln_chain, 1)
                    dve.wait_ge(ln_chain, C * j + 1)
                    nc.vector.memset(carrier[:], 0.0)
                    for t in range(QT):
                        nc.vector.bn_aggr(mv[:, 0, t, :], stats[:, t, :])
                    nc.vector.bn_aggr(mv[0:SC, 0, QT, :], stats[0:SC, QT, :]).then_inc(ln_dve, 1)
                if part == 1:
                    dve.wait_ge(ln_rstd, 4 * j + 2)
                    for t in range(QT):
                        nc.vector.tensor_scalar(z[:, t, :], src[t], mv[:, 0, t, 0:1], rstd[:, 0, t:t + 1],
                                                ALU.subtract, ALU.mult)
                    nc.vector.tensor_scalar(z[0:SC, QT, :], ctx_t[0:SC, :], mv[0:SC, 0, QT, 0:1],
                                            rstd[0:SC, 0, QT:QT + 1], ALU.subtract, ALU.mult).then_inc(ctx_used, 1)
                    dve.wait_ge(ctx_used, j + 1)
                    for t in range(QT):
                        last = nc.vector.bn_stats(stats[:, t, :], z[:, t, :])
                    last.then_inc(ln_chain, 1)
                    dve.wait_ge(ln_chain, C * j + 2)
                    nc.vector.memset(carrier[:], 0.0)
                    for t in range(QT):
                        last = nc.vector.bn_aggr(mv[:, 1, t, :], stats[:, t, :])
                    last.then_inc(ln_dve, 1)
                if part == 2:
                    dve.wait_ge(ln_rstd, 4 * j + 4)
                    for t in range(QT):
                        last = nc.vector.tensor_scalar(z[:, t, :], z[:, t, :], mv[:, 1, t, 0:1],
                                                       rstd[:, 1, t:t + 1], ALU.subtract, ALU.mult)
                    last.then_inc(rows_ready, 1)

            def transposed(bb, j_off, k, v):
                j = bb + j_off
                C = 2 + KD
                n, bank, free, value = filled("L", KD, bb, KD * j_off + k)
                dve.wait_ge(pj_full, n + 1)
                nc.vector.tensor_scalar(lT32[:, k, 0:SQ], bank[:, 0:SQ], gb[:, 2, k:k + 1],
                                        gb[:, 3, k:k + 1], ALU.mult, ALU.add)
                nc.vector.tensor_scalar(lT32[:, k, SQ:SKV], bank[:, SQ:SKV], gb[:, 0, k:k + 1],
                                        gb[:, 1, k:k + 1], ALU.mult, ALU.add).then_inc(free, 1)
                dve.wait_ge(free, value + 1)
                nc.vector.tensor_copy(lT[:, v, 0, k, :], lT32[:, k, :]).then_inc(ln_chain, 1)
                dve.wait_ge(ln_chain, C * j + 3 + k)
                tt(lT[:, v, 1, k, :], lT32[:, k, :], lT[:, v, 0, k, :].bitcast(F32), ALU.subtract).then_inc(lt_ready, 1)

            dve.wait_ge(x_in, 16)
            dve.wait_ge(ln_in, 16 * 4)
            for part in range(3):
                layer_norm(0, part, 0)
            lo = [(wq, k, 0) for k in range(KD)] + [(wkv, k, n) for n in range(2) for k in range(KD)]

            def split_weights(pieces):
                for i in pieces:
                    w, k, n = lo[i]
                    dve.wait_ge(w_hi, i + 1)
                    cols = slice(n * INNER, (n + 1) * INNER)
                    tt(w[:, 1, k, cols], stage[:, i % 2, :], w[:, 0, k, cols].bitcast(F32), ALU.subtract).then_inc(w_lo, 1)

            split_weights(range(2))
            for k in range(KD):
                transposed(0, 0, k, 0)
            split_weights(range(2, 3 * KD))
            nc.vector.tensor_copy(KS[HALF:HALF + 2, :, 0, 1, :],
                                  ident[0:2, 0:1].unsqueeze(2).to_broadcast([2, RING, SKVE]))
            nc.vector.tensor_copy(KS[0:2, :, 1, 1, :],
                                  ident[0:2, 1:2].unsqueeze(2).to_broadcast([2, RING, SKVE])).then_inc(one_rows, 1)
            dve.wait_ge(gates, 1)

            def step(bb, u, has):
                b, p, r = bb + u // PAIRS, u % PAIRS, u % RING
                if has(0):
                    _, bank, free, _ = filled("Q", PAIRS, bb, u)
                    dve.wait_ge(q_hi, PAIRS * bb + u + 1)
                    tt(QS[0:HALF, r, 0, 1, :], bank[0:HALF, 0:SQ], QS[0:HALF, r, 0, 0, :].bitcast(F32), ALU.subtract)
                    tt(QS[HALF:P, r, 1, 1, :], bank[HALF:P, 0:SQ], QS[HALF:P, r, 1, 0, :].bitcast(F32), ALU.subtract
                       ).then_inc(free, 1)
                    _, bank, free, _ = filled("K", PAIRS, bb, u)
                    dve.wait_ge(k_hi, PAIRS * bb + u + 1)
                    tt(KS[HALF:P, r, 0, 0, :], bank[0:HALF, 0:SKVE], KS[0:HALF, r, 0, 0, :].bitcast(F32), ALU.subtract)
                    tt(KS[0:HALF, r, 1, 0, :], bank[HALF:P, 0:SKVE], KS[HALF:P, r, 1, 0, :].bitcast(F32), ALU.subtract
                       ).then_inc(free, 1)
                if exists(b + 1) and exists(b) and p < 3:
                    layer_norm(b + 1, p, 0)
                done = PAIRS - 1 + LAG_Y
                if (u - done - 1) % PAIRS == 0 and has(LAG_Y + 1):
                    j = bb + (u - done - 1) // PAIRS
                    dve.wait_ge(y_full, PAIRS * (j + 1))
                    for t in range(QT):
                        row = X[:, bass.ds(QT * j + t, 1), :].rearrange("p a d -> p (a d)")
                        last = nc.vector.scalar_tensor_tensor(row, yb[:, t * D:(t + 1) * D], tanh_g[:, 0:1], row,
                                                              ALU.mult, ALU.add)
                    last.then_inc(y_read, 1)
                if (u - done - 2) % PAIRS == 0 and has(LAG_Y + 2):
                    j = bb + (u - done - 2) // PAIRS
                    dve.wait_ge(y_read, j + 1)
                    for t in range(QT):
                        n = bass.ds(QT * j + t, 1)
                        nc.vector.bn_stats(h_stats[:, n, :].rearrange("p a s -> p (a s)"),
                                           X[:, n, :].rearrange("p a d -> p (a d)"))
                if has(LAG_NORM):
                    m, v = PAIRS * bb + u - LAG_NORM, (u - LAG_NORM) % 2
                    dve.wait_ge(ov_full, m + 1)
                    nc.vector.reciprocal(inv_sum[:, v, :], ov[:, SQ:2 * SQ]).then_inc(inv_ready, 1)
                    dve.wait_ge(inv_ready, m + 1)
                    if known(m - 1):
                        dve.wait_ge(y_full, m - 1)
                    tt(OT[:, v, :], ov[:, 0:SQ], inv_sum[:, v, :], ALU.mult).then_inc(ot_ready, 1)
                if has(LAG_APX):
                    v = (u - LAG_APX) % 2
                    for i in range(4):
                        n, bank, free, _ = filled("A", 4 * PAIRS, bb, 4 * (u - LAG_APX) + i)
                        dve.wait_ge(st_full, n + 1)
                        nc.vector.tensor_reduce(neg_max[:, v, i // 2, i % 2:i % 2 + 1], bank[:, 0:SKV], AX.X,
                                                ALU.max, negate=True).then_inc(free, 1)
                if exists(b + 1) and exists(b):
                    if p in L_STEPS:
                        transposed(bb, u // PAIRS + 1, L_STEPS[p], (u // PAIRS + 1) % 2)

            pipeline(dve, step)

        @block.tensor
        def _(pe):
            mm = nc.tensor.matmul

            def split3(out, lhs, rhs):
                for k in range(KD):
                    for i, (a, r) in enumerate(((0, 0), (0, 1), (1, 0))):
                        last = mm(out, lhs(a, k), rhs(r, k), start=(k == 0 and i == 0),
                                  stop=(k == KD - 1 and i == 2))
                return last

            def transposes(bb, j_off, k):
                pe.wait_ge(rows_ready, bb + j_off + 1)
                _, bank, free, value = filled("L", KD, bb, KD * j_off + k)
                pe.wait_ge(free, value)
                for t in range(QT):
                    nc.tensor.transpose(bank[:, t * P:(t + 1) * P], z[:, t, k * P:(k + 1) * P], ident[:])
                nc.tensor.transpose(bank[:, SQ:SKV], z[0:SC, QT, k * P:(k + 1) * P],
                                    ident[0:SC, 0:SC]).then_inc(pj_full, 1)

            def step(bb, u, has):
                b, p, r, w = bb + u // PAIRS, u % PAIRS, u % RING, (u // PAIRS) % 2
                first = isinstance(bb, int) and bb == 0 and u == 0

                def scores(i):
                    _, bank, free, value = filled("S", NKT * PAIRS, bb, NKT * (u - LAG_S) + i)
                    m = (u - LAG_S) % RING
                    if i == 0:
                        _, _, mfree, mvalue = filled("M", PAIRS, bb, u - LAG_S)
                        pe.wait_ge(mfree, mvalue + 1)
                    pe.wait_ge(free, value)
                    for half in range(2):
                        head, kt = (i, half) if i < 2 else (half, 2)
                        k0, kn = KT[kt]
                        o = bank[0:kn, half * SQ:(half + 1) * SQ]
                        mm(o, KS[:, m, head, 0, k0:k0 + kn], QS[:, m, head, 0, :], start=True, stop=False)
                        last = mm(o, KS[:, m, head, 1, k0:k0 + kn], QS[:, m, head, 1, :], start=False, stop=True)
                    last.then_inc(st_full, 1)

                if has(0):
                    if p == 0:
                        pe.wait_ge(lt_ready, KD * (b + 1))
                    if first:
                        pe.wait_ge(w_lo, KD)
                    _, bank, free, value = filled("Q", PAIRS, bb, u)
                    pe.wait_ge(free, value)
                    split3(bank[:, 0:SQ], lambda a, k: wq[:, a, k, p * P:(p + 1) * P],
                           lambda a, k: lT[:, w, a, k, 0:SQ]).then_inc(pj_full, 1)
                if has(LAG_S):
                    scores(0)
                if has(0):
                    if first:
                        pe.wait_ge(w_lo, 2 * KD)
                    _, bank, free, value = filled("K", PAIRS, bb, u)
                    pe.wait_ge(free, value)
                    split3(bank[:, 0:SKVE], lambda a, k: wkv[:, a, k, p * P:(p + 1) * P],
                           lambda a, k: lT[:, w, a, k, :]).then_inc(pj_full, 1)
                if has(LAG_S):
                    scores(1)
                if has(LAG_S):
                    scores(2)
                if has(LAG_AV):
                    m, v, q = PAIRS * bb + u - LAG_AV, (u - LAG_AV) % 2, (u - LAG_AV) % PAIRS
                    if known(m):
                        pe.wait_ge(ot_ready, m)
                    part = q // (PAIRS // 2)
                    if q % (PAIRS // 2) == 0:
                        last_v = len(V_STEPS) * ((u - LAG_AV) // PAIRS) + NKT * part + NKT - 1
                        _, _, vfree, vvalue = filled("V", len(V_STEPS), bb, last_v)
                        pe.wait_ge(vfree, vvalue + 1)
                    for kt in range(NKT):
                        kn = KT[kt][1]
                        for half in range(2):
                            slot, col = (half, kt) if kt < 2 else (2, half)
                            _, _, sfree, svalue = filled("S", NKT * PAIRS, bb, NKT * (u - LAG_AV) + slot)
                            pe.wait_ge(sfree, svalue + 1)
                            head = 2 * q + half
                            mm(ov[half * HALF:(half + 1) * HALF, 0:SQ], V[0:kn, kt, head * DH:(head + 1) * DH],
                               probs[0:kn, v, slot, col * SQ:(col + 1) * SQ], start=(kt == 0), stop=(kt == NKT - 1))
                    pe.wait_ge(summed, 2 * m + 2)
                    for half in range(2):
                        last = mm(ov[half * HALF:(half + 1) * HALF, SQ:2 * SQ], ones[:],
                                  prob_sum[:, v, half * SQ:(half + 1) * SQ], start=True, stop=True)
                    last.then_inc(ov_full, 1)
                if p in V_STEPS and has(0):
                    kt, half = V_STEPS[p] % NKT, V_STEPS[p] // NKT
                    k0, kn = KT[kt]
                    if first:
                        pe.wait_ge(w_lo, 3 * KD)
                    _, bank, free, value = filled("V", len(V_STEPS), bb, len(V_STEPS) * (u // PAIRS) + V_STEPS[p])
                    pe.wait_ge(free, value)
                    split3(bank[0:kn, :], lambda a, k: lT[:, w, a, k, k0:k0 + kn],
                           lambda a, k: wkv[:, a, k, INNER + half * 512:INNER + (half + 1) * 512]).then_inc(pj_full, 1)
                if has(LAG_APX):
                    m = (u - LAG_APX) % RING
                    turn = PAIRS // RING
                    pe.wait_ge(q_dup[m], 32 * (turn * bb + (u - LAG_APX) // RING + 1))
                    _, _, kfree, kvalue = filled("K", PAIRS, bb, u - LAG_APX)
                    pe.wait_ge(kfree, kvalue + 1)
                    for i in range(4):
                        head, qt = i // 2, i % 2
                        _, bank, free, value = filled("A", 4 * PAIRS, bb, 4 * (u - LAG_APX) + i)
                        pe.wait_ge(free, value)
                        mm(bank[:, 0:SKVE], QS[:, m, head, 0, qt * P:(qt + 1) * P], KS[:, m, head, 0, :],
                           start=True, stop=True).then_inc(st_full, 1)
                if has(LAG_ROW):
                    _, bank, free, value = filled("M", PAIRS, bb, u - LAG_ROW)
                    pe.wait_ge(free, value)
                    for i in range(4):
                        _, _, afree, avalue = filled("A", 4 * PAIRS, bb, 4 * (u - LAG_ROW) + i)
                        pe.wait_ge(afree, avalue + 1)
                    for qt in range(QT):
                        last = nc.tensor.transpose(bank[0:2, qt * P:(qt + 1) * P],
                                                   neg_max[:, (u - LAG_ROW) % 2, :, qt], ident[:])
                    last.then_inc(pj_full, 1)
                if p in L_STEPS and exists(b + 1) and exists(b):
                    transposes(bb, u // PAIRS + 1, L_STEPS[p])
                if has(LAG_Y):
                    m, v, q = PAIRS * bb + u - LAG_Y, (u - LAG_Y) % 2, (u - LAG_Y) % PAIRS
                    if q == 0 and known(bb + (u - LAG_Y) // PAIRS):
                        pe.wait_ge(y_read, bb + (u - LAG_Y) // PAIRS)
                    pe.wait_ge(ot_ready, m + 1)
                    if isinstance(m, int) and m == 0:
                        pe.wait_ge(wo_in, 16)
                    for t in range(QT):
                        last = mm(yb[:, t * D:(t + 1) * D], OT[:, v, t * P:(t + 1) * P], wo[:, q, :],
                                  start=(q == 0 and t == 0), stop=(q == PAIRS - 1), skip_group_check=True)
                    last.then_inc(y_full, 1)

            pe.wait_ge(tables, 1)
            pe.wait_ge(consts, 6)
            for k in range(KD):
                transposes(0, 0, k)
            pipeline(pe, step)


_INS = ["x", "ctx_1024", "g_xattn", "g_ffn", "L0_xattn_ln1_g", "L0_xattn_ln1_b", "L0_xattn_ln2_g",
        "L0_xattn_ln2_b", "L0_xattn_Wq", "L0_xattn_Wkv", "L0_xattn_Wo", "L0_ffn_router_w",
        "L0_ffn_router_bias", "L0_ffn_expert_gate_w", "L0_ffn_expert_up_w", "L0_ffn_expert_down_w",
        "L0_ffn_conv_w", "L0_ffn_shared_up_w", "L0_ffn_shared_down_w"]


def kernel(**inputs):
    import numpy as np
    import concourse.bacc as bacc
    from concourse.bass_utils import run_bass_kernel_spmd

    nc = bacc.Bacc("TRN2", target_bir_lowering=False, num_devices=1)
    arrays = {f"in_{n}": np.ascontiguousarray(inputs[n]) for n in _INS}
    args = [nc.dram_tensor(n, a.shape, mybir.dt.from_np(a.dtype), kind="ExternalInput").ap()
            for n, a in arrays.items()]
    out = nc.dram_tensor("out", inputs["x"].shape, F32, kind="ExternalOutput").ap()
    build(nc, *args, out)
    return run_bass_kernel_spmd(nc, [arrays], core_ids=[0]).results[0]["out"]
```
